# Optimizing a Trainium2 kernel written in Bass

```python
import numpy as np
import jax
import jax.numpy as jnp

def _softmax(x, axis=-1):
    return jax.nn.softmax(x, axis=axis)

def _gelu(x):
    return jax.nn.gelu(x, approximate=True)

def _silu(x):
    return jax.nn.silu(x)

def _sigmoid(x):
    return jax.nn.sigmoid(x)

def _layernorm(x, axis=-1, eps=1e-05):
    m = jnp.mean(x, axis=axis, keepdims=True)
    v = jnp.var(x, axis=axis, keepdims=True)
    return (x - m) / jnp.sqrt(v + eps)

def _scatter_add(tgt, idx, src, axis=0):
    return tgt.at[idx].add(src)

def _segment_sum(src, seg, n):
    return jax.ops.segment_sum(src, seg, n)
kernel_name = 'mk_vit_tower_cls_d1_tok_img512_r4_f48026'

def setup_inputs(seed: int=0):
    np.random.seed(seed)
    _w = jnp.asarray

    def _rec_inputs():
        import jax
        import jax.numpy as jnp
        _rk = jax.random.key(seed)
        x = 7.22013e-05 + 1.00017 * jax.random.normal(jax.random.fold_in(_rk, 1), (8, 512, 64, 2), jnp.float32)
        cls_tok = 0.02 * jax.random.normal(jax.random.fold_in(_rk, 5), (1, 1, 128), jnp.float32)
        return (x, cls_tok)
    x, cls_tok = _rec_inputs()

    def _L0_tok_setup():
        import jax, jax.numpy as jnp
        import numpy as np
        B, L, C = (8, 512, 64)
        D = C // 8

        def _attn(q, k, v, scale):
            scores = jnp.einsum('bld,bmd->blm', q, k) / scale
            w = jax.nn.softmax(scores, axis=-1)
            return jnp.einsum('blm,bmd->bld', w, v)
        key = jax.random.key(seed)
        ks = jax.random.split(key, 16)
        he = lambda k, cin, cout: jax.random.normal(k, (cin, cout), jnp.float32) * np.sqrt(2.0 / cin)
        inp = {'x': jax.random.normal(ks[0], (B, L, C, 2), jnp.float32)}
        dims = [D, D, C, D, D, C, D, D, C, D, D, C]
        for i, dout in enumerate(dims):
            inp[f'w{i + 1}'] = he(ks[i + 1], C, dout)
        inp['alpha'] = jnp.zeros((1,), jnp.float32)
        inp['gamma'] = jnp.zeros((1,), jnp.float32)
        return inp
    _L0_tok_all = _L0_tok_setup()
    _L0_tok_in = {k: v for k, v in _L0_tok_all.items() if k in ('w1', 'w2', 'w3', 'w4', 'w5', 'w6', 'w7', 'w8', 'w9', 'w10', 'w11', 'w12', 'alpha', 'gamma')}
    del _L0_tok_all

    def _L0_attn_setup():
        import jax, jax.numpy as jnp
        import numpy as np
        B, N, DIM = (4, 512, 128)
        HEADS, DK = (8, 64)
        SCALE = DK ** (-0.5)

        def _split_heads(t, h):
            b, n, hd = t.shape
            return t.reshape(b, n, h, hd // h).transpose(0, 2, 1, 3)
        key = jax.random.key(seed)
        k1, k2, k3, k4 = jax.random.split(key, 4)
        x = jax.random.normal(k1, (B, N, DIM), dtype=jnp.float32)
        Wq = jax.random.normal(k2, (DIM, HEADS * DK), dtype=jnp.float32) * DIM ** (-0.5)
        Wk = jax.random.normal(k3, (DIM, HEADS * DK), dtype=jnp.float32) * DIM ** (-0.5)
        rel_content_bias = jax.random.normal(k4, (1, HEADS, 1, DK), dtype=jnp.float32)
        return {'x': x, 'Wq': Wq, 'Wk': Wk, 'rel_content_bias': rel_content_bias}
    _L0_attn_all = _L0_attn_setup()
    _L0_attn_in = {k: v for k, v in _L0_attn_all.items() if k in ('Wq', 'Wk', 'rel_content_bias')}
    del _L0_attn_all

    def _L0_ffn_setup():
        import jax, jax.numpy as jnp
        import numpy as np
        B, T, D, F, E, K = (8, 256, 128, 512, 8, 2)

        def _moe_forward(x, Wr, br, W1, b1, W2, b2):
            Bx, Tx, Dx = x.shape
            xf = x.reshape(-1, Dx)
            logits = xf @ Wr + br
            probs = jax.nn.softmax(logits, axis=-1)
            vals, idx = jax.lax.top_k(probs, K)
            cw = (jax.nn.one_hot(idx, E, dtype=x.dtype) * vals[..., None]).sum(axis=1)

            def body(acc, params):
                W1e, b1e, W2e, b2e, cwe = params
                h = jax.nn.relu(xf @ W1e + b1e)
                y = h @ W2e + b2e
                return (acc + cwe[:, None] * y, None)
            out, _ = jax.lax.scan(body, jnp.zeros_like(xf), (W1, b1, W2, b2, cw.T))
            return out.reshape(Bx, Tx, Dx)
        key = jax.random.key(seed)
        k0, k1, k2, k3 = jax.random.split(key, 4)
        s_d = 1.0 / np.sqrt(D)
        s_f = 1.0 / np.sqrt(F)
        return {'x': jax.random.normal(k0, (B, T, D), jnp.float32), 'Wr': jax.random.uniform(k1, (D, E), jnp.float32, -s_d, s_d), 'br': jnp.zeros((E,), jnp.float32), 'W1': jax.random.uniform(k2, (E, D, F), jnp.float32, -s_d, s_d), 'b1': jnp.zeros((E, F), jnp.float32), 'W2': jax.random.uniform(k3, (E, F, D), jnp.float32, -s_f, s_f), 'b2': jnp.zeros((E, D), jnp.float32)}
    _L0_ffn_all = _L0_ffn_setup()
    _L0_ffn_in = {k: v for k, v in _L0_ffn_all.items() if k in ('Wr', 'br', 'W1', 'b1', 'W2', 'b2')}
    del _L0_ffn_all
    return {'x': x, 'cls_tok': cls_tok, 'L0_tok_w1': _L0_tok_in['w1'], 'L0_tok_w2': _L0_tok_in['w2'], 'L0_tok_w3': _L0_tok_in['w3'], 'L0_tok_w4': _L0_tok_in['w4'], 'L0_tok_w5': _L0_tok_in['w5'], 'L0_tok_w6': _L0_tok_in['w6'], 'L0_tok_w7': _L0_tok_in['w7'], 'L0_tok_w8': _L0_tok_in['w8'], 'L0_tok_w9': _L0_tok_in['w9'], 'L0_tok_w10': _L0_tok_in['w10'], 'L0_tok_w11': _L0_tok_in['w11'], 'L0_tok_w12': _L0_tok_in['w12'], 'L0_tok_alpha': _L0_tok_in['alpha'], 'L0_tok_gamma': _L0_tok_in['gamma'], 'L0_attn_Wq': _L0_attn_in['Wq'], 'L0_attn_Wk': _L0_attn_in['Wk'], 'L0_attn_rel_content_bias': _L0_attn_in['rel_content_bias'], 'L0_ffn_Wr': _L0_ffn_in['Wr'], 'L0_ffn_br': _L0_ffn_in['br'], 'L0_ffn_W1': _L0_ffn_in['W1'], 'L0_ffn_b1': _L0_ffn_in['b1'], 'L0_ffn_W2': _L0_ffn_in['W2'], 'L0_ffn_b2': _L0_ffn_in['b2']}

def reference(x, cls_tok, L0_tok_w1, L0_tok_w2, L0_tok_w3, L0_tok_w4, L0_tok_w5, L0_tok_w6, L0_tok_w7, L0_tok_w8, L0_tok_w9, L0_tok_w10, L0_tok_w11, L0_tok_w12, L0_tok_alpha, L0_tok_gamma, L0_attn_Wq, L0_attn_Wk, L0_attn_rel_content_bias, L0_ffn_Wr, L0_ffn_br, L0_ffn_W1, L0_ffn_b1, L0_ffn_W2, L0_ffn_b2):
    import jax
    import jax.numpy as jnp

    def _L0_tok_ref(x, w1, w2, w3, w4, w5, w6, w7, w8, w9, w10, w11, w12, alpha, gamma):
        import jax, jax.numpy as jnp
        import numpy as np
        B, L, C = (8, 512, 64)
        D = C // 8

        def _attn(q, k, v, scale):
            scores = jnp.einsum('bld,bmd->blm', q, k) / scale
            w = jax.nn.softmax(scores, axis=-1)
            return jnp.einsum('blm,bmd->bld', w, v)
        ecg = x[:, :, :, 0]
        pcg = x[:, :, :, 1]
        proj = lambda f, w: jnp.einsum('blc,cd->bld', f, w)
        scale = jnp.sqrt(jnp.asarray(D, x.dtype))
        qkv_ecg_intra = _attn(proj(ecg, w1), proj(ecg, w2), proj(ecg, w3), scale)
        qkv_ecg_inter = _attn(proj(ecg, w4), proj(pcg, w5), proj(pcg, w6), scale)
        ecg_out = qkv_ecg_inter + alpha * qkv_ecg_intra
        qkv_pcg_intra = _attn(proj(pcg, w7), proj(pcg, w8), proj(pcg, w9), scale)
        qkv_pcg_inter = _attn(proj(pcg, w10), proj(ecg, w11), proj(ecg, w12), scale)
        pcg_out = qkv_pcg_inter + gamma * qkv_pcg_intra
        return jnp.concatenate([ecg_out, pcg_out], axis=-1)

    def _L0_attn_ref(x, Wq, Wk, rel_content_bias):
        import jax, jax.numpy as jnp
        import numpy as np
        B, N, DIM = (4, 512, 128)
        HEADS, DK = (8, 64)
        SCALE = DK ** (-0.5)

        def _split_heads(t, h):
            b, n, hd = t.shape
            return t.reshape(b, n, h, hd // h).transpose(0, 2, 1, 3)
        q = _split_heads(x @ Wq, HEADS) * SCALE
        k = _split_heads(x @ Wk, HEADS)
        v = _split_heads(x, HEADS)
        logits = jnp.einsum('bhid,bhjd->bhij', q + rel_content_bias, k)
        attn = jax.nn.sigmoid(logits)
        out = jnp.einsum('bhij,bhjd->bhid', attn, v)
        b, h, n, d = out.shape
        return out.transpose(0, 2, 1, 3).reshape(b, n, h * d)

    def _L0_ffn_ref(x, Wr, br, W1, b1, W2, b2):
        import jax, jax.numpy as jnp
        import numpy as np
        B, T, D, F, E, K = (8, 256, 128, 512, 8, 2)

        def _moe_forward(x, Wr, br, W1, b1, W2, b2):
            Bx, Tx, Dx = x.shape
            xf = x.reshape(-1, Dx)
            logits = xf @ Wr + br
            probs = jax.nn.softmax(logits, axis=-1)
            vals, idx = jax.lax.top_k(probs, K)
            cw = (jax.nn.one_hot(idx, E, dtype=x.dtype) * vals[..., None]).sum(axis=1)

            def body(acc, params):
                W1e, b1e, W2e, b2e, cwe = params
                h = jax.nn.relu(xf @ W1e + b1e)
                y = h @ W2e + b2e
                return (acc + cwe[:, None] * y, None)
            out, _ = jax.lax.scan(body, jnp.zeros_like(xf), (W1, b1, W2, b2, cw.T))
            return out.reshape(Bx, Tx, Dx)
        return _moe_forward(x, Wr, br, W1, b1, W2, b2)
    h = _L0_tok_ref(x, L0_tok_w1, L0_tok_w2, L0_tok_w3, L0_tok_w4, L0_tok_w5, L0_tok_w6, L0_tok_w7, L0_tok_w8, L0_tok_w9, L0_tok_w10, L0_tok_w11, L0_tok_w12, L0_tok_alpha, L0_tok_gamma)
    h = jnp.concatenate([jnp.broadcast_to(cls_tok, (h.shape[0], 1, h.shape[2])), h], axis=1)
    h = h + _L0_attn_ref(_layernorm(h, axis=-1), L0_attn_Wq, L0_attn_Wk, L0_attn_rel_content_bias)
    h = h + _L0_ffn_ref(_layernorm(h, axis=-1), L0_ffn_Wr, L0_ffn_br, L0_ffn_W1, L0_ffn_b1, L0_ffn_W2, L0_ffn_b2)
    return h

_drawn_inputs = setup_inputs


def setup_inputs(seed=0):
    import zlib

    import numpy as np

    out = dict(_drawn_inputs(seed))
    spreads = {'L0_ffn_br': (0.0, 0.8), 'L0_ffn_b1': (0.0, 0.8), 'L0_ffn_b2': (0.0, 0.8)}
    factors = {'cls_tok': 5.609, 'L0_ffn_Wr': 8.0, 'L0_ffn_W1': 8.0, 'L0_ffn_W2': 8.0}
    for name, (base, spread) in spreads.items():
        noise = np.random.default_rng([zlib.crc32(name.encode()), seed]).standard_normal(out[name].shape)
        drawn = base * np.exp(spread * noise) if base else spread * noise
        out[name] = jnp.asarray(drawn.astype(out[name].dtype))
    for name, factor in factors.items():
        out[name] = (out[name] * factor).astype(out[name].dtype)
    return out
```

```python
from contextlib import ExitStack

import numpy as np

import concourse.bass as bass
from concourse import mybir

B, L, C = 8, 512, 64
D = 2 * C
DQ = C // 8
ATT = 4
H, DK = 8, 64
DV = D // H
EX, F = 8, 512
P = 128
LT = L // P
FB = F // P
LN_EPS = 1e-5

F32 = mybir.dt.float32
F32R = mybir.dt.float32r
U32 = mybir.dt.uint32
ACT = mybir.ActivationFunctionType
ALU = mybir.AluOpType
AX_X = mybir.AxisListType.X

ROWS = 32
SHIFT = 3 * DQ
VW = C + 2

C_ID, C_SEL, C_HALF, C_IOTA = 0, P, 3 * P, 4 * P
C_MQ, C_MK, C_ONE, C_NHALF = C_IOTA + EX, C_IOTA + EX + 1, C_IOTA + EX + 2, C_IOTA + EX + 3
C_HOT = C_NHALF + 1
C_W = C_HOT + EX * B


def constants():
    c = np.zeros((P, C_W), np.float32)
    c[:, C_ID:C_ID + P] = np.eye(P)
    for h in range(H):
        for part in range(2):
            for d in range(DV):
                c[(h % 4) * 2 * DV + part * DV + d, C_SEL + (h // 4) * P + h * DV + d] = 0.5
    c[:, C_HALF:C_HALF + P] = 0.5 * np.eye(P)
    c[:, C_IOTA:C_IOTA + EX] = np.arange(EX)
    for a in range(ATT):
        r = a * ROWS
        c[r + DQ:r + 2 * DQ, C_MQ] = -1.0
        c[r + SHIFT + 1, C_MQ] = -1.0
        c[r + 2 * DQ:r + 3 * DQ, C_MK] = -1.0
        c[r + SHIFT:r + SHIFT + 2, C_MK] = 1.0
        c[r + SHIFT:r + SHIFT + 2, C_ONE] = 1.0
    c[:, C_NHALF] = -0.5
    for e in range(EX):
        c[e, C_HOT + e * B:C_HOT + (e + 1) * B] = 1.0
    return c


N_MAX, N_EXP, N_TANH, N_RELU = 2 * LT, 2 * ATT, 2 * H, 2 * EX
ELEMENT_KINDS = ("exp", "tanh", "relu")
LAG = 2
ATTN_LINKS = 27


def attention_steps():
    s = [("proj", 0)] + [("max", i) for i in range(N_MAX)] + [("shift", 0)]
    s += [("exp", i) for i in range(N_EXP)] + [("norm", 0), ("ln1", 0), ("gates", 0)]
    s += [("g", 0)]
    for h in range(H):
        s += [("g", h + 1)] * (h + 1 < H) + [("tanh", 2 * h), ("tanh", 2 * h + 1)]
    s += [("mix", 0), ("route", 0)]
    return s


def expert_steps():
    return [("relu", i) for i in range(N_RELU)] + [("fin", 0)]


def with_uses(steps, lag):
    out, waiting = [], []
    for s in steps:
        if s[0] in ELEMENT_KINDS:
            out.append(s)
            waiting.append(s)
            if len(waiting) > lag:
                out.append(("use", waiting.pop(0)))
            continue
        needs = {"norm": ("exp",), "mix": ("tanh",), "fin": ("relu",)}.get(s[0], ())
        while any(w[0] in needs for w in waiting):
            out.append(("use", waiting.pop(0)))
        out.append(s)
    return out + [("use", w) for w in waiting]


def merge(a, e):
    out, k = [], 0
    for s in a:
        if s[0] == "mix":
            out += e[k:]
            k = len(e)
        out.append(s)
        if s[0] in ("max", "tanh", "exp") and s[1] % 2 == 1 and k < len(e):
            out += e[k:k + 1]
            k += 1
    return out


def build(nc, A):
    with ExitStack() as ctx:
        def sb(name, shape, dt=F32):
            return ctx.enter_context(nc.sbuf_tensor(name, shape, dt))

        def sem(name):
            return ctx.enter_context(nc.semaphore(name))

        con = sb("con", [P, C_W])
        wqk = sb("wqk", [P, 2 * P])
        wv = sb("wv", [P, ATT * C])
        wqT = sb("wqT", [DK, H, P])
        wkT = sb("wkT", [DK, H, P])
        wr = sb("wr", [P, EX])
        brb = sb("brb", [P, EX])
        ag = sb("ag", [P, 2])
        b1T = sb("b1T", [P, EX * FB])
        b2T = sb("b2T", [P, EX])
        b1e = sb("b1e", [EX, F])
        b2e = sb("b2e", [EX, D])
        biasT = sb("biasT", [DK, H])
        clsr = sb("clsr", [B, D])
        clsx = sb("clsx", [B, D])
        w1h, w1l = sb("w1h", [P, EX, F], F32R), sb("w1l", [P, EX, F], F32R)
        w2h, w2l = sb("w2h", [P, EX, F], F32R), sb("w2l", [P, EX, F], F32R)
        mh, ml = sb("mh", [P, H, P], F32R), sb("ml", [P, H, P], F32R)
        u = sb("u", [P, H])
        rrep, grep = sb("rrep", [P, P]), sb("grep", [P, P])
        kc = sb("kc", [DK, H])
        cc = sb("cc", [P, 24])
        xin = sb("xin", [P, L])
        trnd = sb("trnd", [P, L], F32R)
        kz = sb("kz", [P, ATT, L], F32R)
        qs = sb("qs", [P, L], F32R)
        v1h, v1l = sb("v1h", [P, LT * ATT, VW], F32R), sb("v1l", [P, LT * ATT, VW], F32R)
        nm = sb("nm", [P, LT, P])
        e = sb("e", [P, 2, 2 * L])
        eh, el = sb("eh", [P, 2, 2 * L], F32R), sb("el", [P, 2, 2 * L], F32R)
        ot = sb("ot", [P, ATT, L])
        h1, h2 = sb("h1", [P, LT, D]), sb("h2", [P, LT, D])
        x = sb("x", [P, LT, D])
        xT = sb("xT", [P, L])
        xh, xl = sb("xh", [P, L], F32R), sb("xl", [P, L], F32R)
        yh, yl = sb("yh", [P, L], F32R), sb("yl", [P, L], F32R)
        vz = sb("vz", [P, LT, H, P], F32R)
        gf = sb("gf", [P, L])
        gh, gl = sb("gh", [P, 2, L], F32R), sb("gl", [P, 2, L], F32R)
        tk, tq = sb("tk", [P, L]), sb("tq", [P, L])
        sm = sb("sm", [P, 192])
        mx8 = sb("mx8", [P, LT, 8])
        ix8 = sb("ix8", [P, LT, 8], U32)
        rt = sb("rt", [P, 4, LT, EX])
        cwT = sb("cwT", [EX, L])
        mo = sb("mo", [P, 4, L])
        acc = sb("acc", [P, L])
        outs = sb("outs", [P, LT, D])
        colc = sb("colc", [P, B])
        tl = sb("tl", [P, B])
        tr2 = sb("tr2", [P, 2, B], F32R)
        cwd = nc.dram_tensor("cwd", [EX, L], F32).ap()

        W = ctx.enter_context(nc.psum_tensor("W", [P, 4, L], F32))
        AC = ctx.enter_context(nc.psum_tensor("AC", [P, 2, L], F32))
        M = ctx.enter_context(nc.psum_tensor("M", [P, L], F32))
        Y = ctx.enter_context(nc.psum_tensor("Y", [P, L], F32))

        ident = con[:, C_ID:C_ID + P]
        AT = ot[:, 0:2, :]
        cwb, prod = mo[:, 0:2, :], mo[:, 2:4, :]
        ez = e[:].rearrange("p s (k n) -> p (s k) n", k=2)
        hc = x[0:B, 2, :]
        xcT, xch, xcl = tl[:], tr2[:, 0, :], tr2[:, 1, :]
        SMALL = ((con, "consts"), (wqk, "wqk"), (wv, "wv"), (wqT, "wqT"), (wkT, "wkT"), (wr, "wr"), (brb, "brb"),
                 (ag, "ag"), (b1T, "b1T"), (b2T, "b2T"), (b1e, "b1"), (b2e, "b2"), (biasT, "biasT"),
                 (clsr, "cls"), (xT, "wk"))

        consts_in = sem("consts_in")
        wts_in = [sem(f"wts_in{i}") for i in range(4)]
        wts_hi = sem("wts_hi")
        wts_lo = sem("wts_lo")
        pool_set = sem("pool_set")
        setup_pe, setup_dve, setup_act = sem("setup_pe"), sem("setup_dve"), sem("setup_act")
        xin_ready = sem("xin_ready")
        w_ready = sem("w_ready")
        w_read = [sem("w_read0"), sem("w_read1")]
        m_ready = sem("m_ready")
        m_read = sem("m_read")
        ac_read = [sem("ac_read0"), sem("ac_read1")]
        hi_ready = sem("hi_ready")
        parts_ready = sem("parts_ready")
        parts_used = sem("parts_used")
        rounded = sem("rounded")
        shift_ready = sem("shift_ready")
        var_ready = sem("var_ready")
        rstd_ready = sem("rstd_ready")
        x_ready = sem("x_ready")
        vz_hi, vz_ready = sem("vz_hi"), sem("vz_ready")
        xp_ready = sem("xp_ready")
        yp_ready = sem("yp_ready")
        g_ready = sem("g_ready")
        ck_ready = sem("ck_ready")
        logits_ready = sem("logits_ready")
        ex_ready = sem("ex_ready")
        cw_ready = sem("cw_ready")
        cwd_done = sem("cwd_done")
        cwb_ready = [sem("cwb_ready0"), sem("cwb_ready1")]
        prod_ready = sem("prod_ready")
        acc_added = sem("acc_added")
        fin_ready = sem("fin_ready")
        out_ready = sem("out_ready")
        out_done = sem("out_done")
        carried = sem("carried")
        chain = sem("chain")
        tail_pe, tail_act, tail_pool, tail_done = sem("tail_pe"), sem("tail_act"), sem("tail_pool"), sem("tail_done")
        tail_dve, tail_z, tail_t, tail_x = sem("tail_dve"), sem("tail_z"), sem("tail_t"), sem("tail_x")
        tail_dve_l, tail_dve_w, tail_cols = sem("tail_dve_l"), sem("tail_dve_w"), sem("tail_cols")

        credit = [(prod_ready, 2), (acc_added, 2), (out_ready, 1), (fin_ready, 1), (out_done, 16)]

        def wait(eng, s, n, per, k):
            k += sum(c for t, c in credit if t is s)
            if isinstance(n, int):
                if n * per + k > 0:
                    eng.wait_ge(s, n * per + k)
            else:
                eng.wait_ge(s, n * per + k)

        first = with_uses(attention_steps(), LAG)
        both = with_uses(merge(attention_steps(), expert_steps()), LAG)
        last = with_uses(expert_steps(), LAG)
        W_KINDS = {"proj": 2, "max": 1, "norm": 2, "exp": 1, "tanh": 1, "relu": 1}
        E_KINDS = {k: 1 for k in ELEMENT_KINDS}

        def positions(steps, takes):
            at, k = {}, 0
            for s in steps:
                if takes.get(s[0], 0):
                    at[s] = k
                    k += takes[s[0]]
            return at, k

        (W1, NW1), (E1, NE1) = positions(first, W_KINDS), positions(first, E_KINDS)
        (W2, NW), (E2, NE) = positions(both, W_KINDS), positions(both, E_KINDS)
        (W3, _), (E3, _) = positions(last, W_KINDS), positions(last, E_KINDS)
        assert NW1 % 2 == NW % 2 == NE1 % 2 == NE % 2 == 0

        class Round:

            def __init__(self, steps, n, m, w_at, e_at, full, w0, e0):
                self.steps, self.n, self.m = steps, n, m
                self.w_at, self.e_at, self.full, self.w0, self.e0 = w_at, e_at, full, w0, e0

            def slot(self, step, j=0):
                return (self.w_at[step] + j) % 2

            def eslot(self, step):
                return self.e_at[step] % 2

            def wait_full(self, eng, step, j=0):
                wait(eng, w_ready, self.full, NW, self.w0 + self.w_at[step] + j + 1)

            def wait_read(self, eng, step, j=0, before=0):
                k = self.w0 + self.w_at[step] + j
                wait(eng, w_read[k % 2], self.full, NW // 2, k // 2 + 1 - before)

            def wait_e(self, eng, s, step, before=0):
                wait(eng, s, self.full, NE, self.e0 + self.e_at[step] + 1 - before)

        def rounds(eng, body):
            body(Round(first, 0, None, W1, E1, 0, 0, 0))
            with eng.Fori(1, B) as b:
                body(Round(both, b, b - 1, W2, E2, b - 1, NW1, NE1))
            body(Round(last, None, B - 1, W3, E3, B - 1, NW1, NE1))

        def apart(eng):
            eng.sem_inc(carried, 1)

        MU = {"q": 1, "qs": 2, "xT": 3, "tk": 4, "tq": 5, "g": 6, "mix": 14, "yT": 15, "logits": 16, "cwT": 17}
        NM = 17
        XC, BK, TCC, CCX, T1, LOGIT = 0, 1, 2, 3, 4, 5
        VAR, RSTD, MV, BN = 8, 9, 10, 12
        S_BN, S_MV, S_VE, S_RS, S_DEN, S_MX, S_SX, S_ST, S_SB, S_R = 0, 24, 32, 36, 48, 64, 80, 81, 82, 96
        nhalf = con[:, C_NHALF:C_NHALF + 1]
        m32 = e[:, 0, :].rearrange("p (h d) -> p h d", h=H)
        urep = e[:, 1, 0:P]

        block = ctx.enter_context(nc.Block())

        @block.sync
        def _(sp):
            sp.sem_inc(out_done, 16)
            for dst, src in SMALL:
                sp.dma_start(dst[:], A[src]).then_inc(consts_in, 16)
            sp.dma_start(xin[:], A["xT"][0]).then_inc(xin_ready, 16)
            for c in range(2 * EX):
                if c >= 4:
                    sp.wait_ge(wts_lo, c - 3)
                src = A["w1"][:, c, :] if c < EX else A["w2"][:, c - EX, :]
                sp.dma_start(mo[:, c % 4, :], src).then_inc(wts_in[c % 4], 16)
            sp.wait_ge(wts_lo, 2 * EX)

            def body(r):
                n, m = r.n, r.m
                for s in r.steps:
                    if s[0] == "proj" and s[1] == 0 and n is not None:
                        r.wait_full(sp, s, 1)
                        if isinstance(n, int):
                            sp.dma_start(xin[:], A["xT"][n + 1]).then_inc(xin_ready, 16)
                        else:
                            sp.dma_start(xin[:], A["xT"][bass.ds(n + 1, 1)].rearrange("a p n -> p (a n)")
                                         ).then_inc(xin_ready, 16)
                    if s[0] == "relu" and s[1] % 2 == 0:
                        ex = s[1] // 2
                        wait(sp, cwd_done, m, 16, 16)
                        apart(sp)
                        wait(sp, prod_ready, m, EX, ex - 1)
                        sp.dma_start(cwb[:, ex % 2, :], cwd[ex:ex + 1, :].partition_broadcast(P)
                                     ).then_inc(cwb_ready[ex % 2], 16)
                    if s[0] == "fin":
                        wait(sp, out_ready, m, 1, 1)
                        if isinstance(m, int):
                            dst = A["out"][m, 1:L + 1, :].rearrange("(t p) d -> p t d", p=P)
                        else:
                            dst = A["out"][bass.ds(m, 1), 1:L + 1, :].rearrange("a (t p) d -> p (a t) d", p=P)
                        sp.dma_start(dst, outs[:]).then_inc(out_done, 16)
                    if s[0] == "route":
                        wait(sp, m_read, n, NM, MU["cwT"])
                        if m is not None:
                            for k in range(2):
                                wait(sp, cwb_ready[k], m, 8 * EX, 8 * EX)
                        sp.dma_start(cwd, cwT[:]).then_inc(cwd_done, 16)

            rounds(sp, body)
            sp.wait_ge(tail_dve, 1)
            sp.dma_start(A["out"][:, 0, :], x[0:B, 3, :]).then_inc(tail_done, 16)
            sp.wait_ge(tail_done, 16)
            sp.wait_ge(out_done, 16 * (B + 1))
            sp.wait_ge(xin_ready, 16 * (B + 1))

        @block.gpsimd
        def _(pool):
            g = nc.gpsimd
            pool.sem_inc(acc_added, 2)
            g.memset(nm[:], 0.0)
            g.memset(kz[:].bitcast(F32), 0.0)
            g.memset(v1h[:].bitcast(F32), 1.0)
            g.memset(v1l[:].bitcast(F32), 0.0)
            g.memset(vz[:].bitcast(F32), 0.0).then_inc(pool_set, 1)
            pool.wait_ge(consts_in, 16 * len(SMALL))
            pool.wait_ge(var_ready, 1)
            g.tensor_tensor(cc[0:B, RSTD:RSTD + 1], cc[0:B, VAR:VAR + 1], nhalf[0:B], ALU.pow).then_inc(rstd_ready, 1)

            def split_weights(c):
                pool.wait_ge(wts_hi, c + 1)
                hi, lo = (w1h, w1l) if c < EX else (w2h, w2l)
                g.tensor_tensor(lo[:, c % EX, :], mo[:, c % 4, :], hi[:, c % EX, :], ALU.subtract).then_inc(wts_lo, 1)

            def rstd(n, k):
                wait(pool, var_ready, n, 2, k + 1)
                g.tensor_tensor(sm[:, S_RS:S_RS + LT], sm[:, S_VE:S_VE + LT], nhalf.to_broadcast([P, LT]),
                                ALU.pow).then_inc(rstd_ready, 1)

            def values(n):
                wait(pool, x_ready, n, 2, 1)
                if not isinstance(n, int):
                    wait(pool, m_read, n, NM, 0)
                    apart(pool)
                for lo in range(2):
                    for t in range(LT):
                        xv = x[:, t, :].rearrange("p (k q d) -> p k q d", k=2, q=4)
                        v = vz[:, t, :, :].rearrange("p (k q) c -> p k (q c)", k=2)
                        for q in range(4):
                            at = q * P + q * 2 * DV
                            if lo:
                                ins = g.tensor_tensor(v[:, :, at + DV:at + 2 * DV], xv[:, :, q, :],
                                                      v[:, :, at:at + DV], ALU.subtract)
                            else:
                                ins = g.tensor_copy(v[:, :, at:at + DV], xv[:, :, q, :])
                    if lo:
                        ins.then_inc(vz_ready, 1)
                    else:
                        ins.then_inc(vz_hi, 1)
                        wait(pool, vz_hi, n, 1, 1)

            def body(r):
                wsplit = 0
                for s in r.steps:
                    if r.m is None and s[0] in ("max", "tanh") and wsplit < 2 * EX:
                        split_weights(wsplit)
                        wsplit += 1
                    if s[0] == "ln1":
                        rstd(r.n, 1)
                        values(r.n)
                    if s[0] == "mix":
                        rstd(r.n, 2)
                    if s[0] == "use" and s[1][0] == "relu" and s[1][1] % 2 == 1:
                        ex = s[1][1] // 2
                        wait(pool, prod_ready, r.m, EX, ex + 1)
                        if ex == 0:
                            wait(pool, fin_ready, r.m, 1, 0)
                            apart(pool)
                            g.tensor_copy(acc[:], prod[:, 0, :]).then_inc(acc_added, 1)
                        else:
                            wait(pool, acc_added, r.m, EX, ex)
                            g.tensor_tensor(acc[:], acc[:], prod[:, ex % 2, :], ALU.add).then_inc(acc_added, 1)

            rounds(pool, body)
            wait(pool, var_ready, B, 2, 2)
            g.tensor_tensor(cc[0:B, RSTD:RSTD + 1], cc[0:B, VAR:VAR + 1], nhalf[0:B], ALU.pow).then_inc(tail_pool, 1)

        @block.scalar
        def _(act):
            a = nc.scalar
            act.wait_ge(setup_dve, 6)
            a.activation(cc[:, TCC:TCC + 1], cc[:, LOGIT:LOGIT + 1], ACT.Tanh, scale=0.5).then_inc(setup_act, 1)

            def split_weights(c):
                act.wait_ge(wts_in[c % 4], 16 * (c // 4 + 1))
                a.copy((w1h if c < EX else w2h)[:, c % EX, :], mo[:, c % 4, :]).then_inc(wts_hi, 1)

            def elements(r, s):
                kind, i = s
                slot, es = r.slot(s), r.eslot(s)
                src = W[:, 2 * slot:2 * slot + 2, :]
                dst = e[:, es, :].rearrange("p (k n) -> p k n", k=2)
                dh = eh[:, es, :].rearrange("p (k n) -> p k n", k=2)
                r.wait_full(act, s)
                r.wait_e(act, parts_ready, s, 2)
                if kind == "tanh":
                    a.activation(dst, src, ACT.Tanh, scale=0.5).then_inc(w_read[slot], 1)
                elif kind == "exp":
                    a.activation(dst, src, ACT.Exp, scale=float(DQ) ** -0.5)
                    r.wait_e(act, parts_used, s, 2)
                    a.activation(dh, src, ACT.Exp, scale=float(DQ) ** -0.5).then_inc(w_read[slot], 1)
                else:
                    for k in range(2):
                        a.activation(dst[:, k, :], src[:, k, :], ACT.Relu, bias=b1T[:, 2 * i + k:2 * i + k + 1])
                    r.wait_e(act, parts_used, s, 2)
                    for k in range(2):
                        ins = a.activation(dh[:, k, :], src[:, k, :], ACT.Relu, bias=b1T[:, 2 * i + k:2 * i + k + 1])
                    ins.then_inc(w_read[slot], 1)

            def body(r):
                n = r.n
                wsplit = 0
                for s in r.steps:
                    if s[0] in ELEMENT_KINDS:
                        elements(r, s)
                    elif s[0] == "use" and s[1][0] == "exp" and s[1][1] % 2 == 1:
                        at = s[1][1] // 2
                        r.wait_e(act, parts_used, s[1])
                        if at == 0 and not isinstance(n, int):
                            wait(act, m_ready, n, NM, MU["mix"] - NM)
                        a.copy(ot[0:C + 1, at, :], AC[0:C + 1, at % 2, :]).then_inc(ac_read[at % 2], 1)
                    elif s[0] == "use" and s[1][0] == "tanh" and s[1][1] in (H - 1, 2 * H - 1):
                        k = s[1][1] // H
                        r.wait_e(act, parts_used, s[1])
                        a.copy(AT[:, k, :], AC[:, k, :]).then_inc(ac_read[k], 1)
                    elif s[0] == "proj":
                        r.wait_full(act, s)
                        if not isinstance(n, int):
                            wait(act, m_read, n, NM, MU["qs"] - NM)
                        a.activation(trnd[:], W[:, 2 * r.slot(s), :], ACT.Identity,
                                     bias=con[:, C_ONE:C_ONE + 1]).then_inc(rounded, 1)
                        wait(act, m_ready, n, NM, MU["q"])
                        r.wait_read(act, s)
                        a.copy(trnd[:], M[:]).then_inc(rounded, 1)
                    elif s[0] == "shift":
                        wait(act, m_ready, n, NM, MU["qs"])
                        a.copy(trnd[:], M[:]).then_inc(rounded, 1)
                    elif s[0] == "ln1":
                        wait(act, m_ready, n, NM, MU["xT"])
                        a.activation(xT[:], M[:], ACT.Identity, accum_out=sm[:, S_SX:S_SX + 1]).then_inc(m_read, 1)
                    elif s[0] == "gates":
                        wait(act, m_ready, n, NM, MU["tk"])
                        if not isinstance(n, int):
                            pass
                        a.activation(tk[:], M[:], ACT.Tanh, scale=0.5, bias=cc[:, BK:BK + 1]).then_inc(m_read, 1)
                        wait(act, m_ready, n, NM, MU["tq"])
                        a.activation(tq[:], M[:], ACT.Tanh, scale=0.5).then_inc(m_read, 1)
                    elif s[0] == "g":
                        h = s[1]
                        wait(act, m_ready, n, NM, MU["g"] + h)
                        wait(act, g_ready, n, H, h)
                        a.activation(gf[:], M[:], ACT.Identity, bias=u[:, h:h + 1]).then_inc(m_read, 1)
                    elif s[0] == "mix":
                        wait(act, m_ready, n, NM, MU["yT"])
                        a.copy(xT[:], M[:]).then_inc(m_read, 1)
                    elif s[0] == "route":
                        wait(act, logits_ready, n, 1, 1)
                        a.activation(rt[:, 1, :, :], rt[:, 0, :, :], ACT.Exp).then_inc(ex_ready, 1)
                        wait(act, m_ready, n, NM, MU["cwT"])
                        wait(act, cwd_done, n, 16, 0)
                        a.copy(cwT[:], M[0:EX, :]).then_inc(m_read, 1)
                    if r.m is None and s[0] in ("max", "tanh") and wsplit < 2 * EX:
                        split_weights(wsplit)
                        wsplit += 1
                if r.m is None:
                    assert wsplit == 2 * EX

            rounds(act, body)
            act.wait_ge(tail_dve_l, 1)
            a.activation(rt[0:B, 1, 0, :], rt[0:B, 0, 0, :], ACT.Exp).then_inc(tail_act, 1)
            act.wait_ge(tail_dve_w, 1)
            for ex in range(EX):
                act.wait_ge(tail_z, ex + 1)
                if ex >= 4:
                    act.wait_ge(tail_t, ex - 3)
                a.activation(ez[0:B, ex % 4, :], W[0:B, ex % 4, :], ACT.Relu,
                             scale=rt[0:B, 0, 0, ex:ex + 1]).then_inc(tail_act, 1)

        @block.vector
        def _(dve):
            v = nc.vector
            dve.sem_inc(prod_ready, 2)
            dve.sem_inc(out_ready, 1)
            links = [0]

            def link(ins, n=0, per=0):
                links[0] += 1
                ins.then_inc(chain, 1)
                wait(dve, chain, n, per, links[0])

            def layer_norm(src, dst, tiles, n, per, k_rstd, rows=P, bn=None, mv=None, ve=None, rs=None,
                           rstd=rstd_ready, n_rstd=None, per_rstd=0):
                for t in range(tiles):
                    ins = v.bn_stats(bn[0:rows, 6 * t:6 * t + 6], src(t))
                link(ins, n, per)
                apart(dve)
                for t in range(tiles):
                    ins = v.bn_aggr(mv[0:rows, 2 * t:2 * t + 2], bn[0:rows, 6 * t:6 * t + 6])
                link(ins, n, per)
                v.tensor_scalar(ve[0:rows, 0:tiles], mv[0:rows, 1:2 * tiles:2], LN_EPS, None, ALU.add
                                ).then_inc(var_ready, 1)
                wait(dve, rstd, n_rstd, per_rstd, k_rstd)
                for t in range(tiles):
                    ins = v.tensor_scalar(dst(t), src(t), mv[0:rows, 2 * t:2 * t + 1], rs[0:rows, t:t + 1],
                                          ALU.subtract, ALU.mult)
                return ins

            def top2(rows, T, n, per, exp_sem, n_e, per_e, k_e, lg_sem):
                r0, r1, r2, r3 = (rt[0:rows, i, 0:T, :] for i in range(4))
                mxs, den = sm[0:rows, S_MX:S_MX + T], sm[0:rows, S_R:S_R + T]
                link(v.tensor_reduce(mxs, r0, AX_X, ALU.max), n, per)
                v.tensor_tensor(r0, r0, mxs.unsqueeze(2).to_broadcast([rows, T, EX]), ALU.subtract
                                ).then_inc(lg_sem, 1)
                wait(dve, exp_sem, n_e, per_e, k_e)
                link(v.tensor_reduce(den, r1, AX_X, ALU.add), n, per)
                link(v.reciprocal(den, den), n, per)
                link(v.tensor_tensor(r1, r1, den.unsqueeze(2).to_broadcast([rows, T, EX]), ALU.mult), n, per)
                apart(dve)
                for t in range(T):
                    ins = v.max(mx8[0:rows, t, :], rt[0:rows, 1, t, :])
                link(ins, n, per)
                apart(dve)
                for t in range(T):
                    ins = v.max_index(ix8[0:rows, t, :], mx8[0:rows, t, :], rt[0:rows, 1, t, :])
                link(ins, n, per)
                iota = con[0:rows, C_IOTA:C_IOTA + EX].unsqueeze(1).to_broadcast([rows, T, EX])
                v.tensor_tensor(r2, iota, ix8[0:rows, 0:T, 0:1].to_broadcast([rows, T, EX]), ALU.is_equal)
                link(v.tensor_tensor(r3, iota, ix8[0:rows, 0:T, 1:2].to_broadcast([rows, T, EX]), ALU.is_equal),
                     n, per)
                link(v.tensor_tensor(r2, r2, r3, ALU.add), n, per)
                return v.tensor_tensor(r0, r2, r1, ALU.mult)

            dve.wait_ge(consts_in, 16 * len(SMALL))
            ins = layer_norm(lambda t: clsr[:], lambda t: clsx[:], 1, 0, 0, 1, rows=B, bn=cc[:, BN:BN + 6],
                             mv=cc[:, MV:MV + 2], ve=cc[:, VAR:VAR + 1], rs=cc[:, RSTD:RSTD + 1],
                             n_rstd=0, per_rstd=0)
            ins.then_inc(setup_dve, 1)
            dve.wait_ge(setup_pe, 2)
            for k in range(2):
                ins = v.tensor_scalar(m32[:, 4 * k:4 * k + 4, :], AC[:, k, :].rearrange("p (h d) -> p h d", h=4),
                                      float(DK) ** -0.5, None, ALU.mult)
            v.tensor_copy(u[:], Y[:, 0:H])
            link(v.tensor_copy(sm[:, 0:1], con[:, 0:1]))
            v.tensor_copy(urep.rearrange("p (h d) -> p h d", h=H), u[:].unsqueeze(2).to_broadcast([P, H, DV]))
            link(v.tensor_copy(mh[:], m32))
            v.tensor_tensor(ml[:], m32, mh[:], ALU.subtract).then_inc(setup_dve, 1)
            dve.wait_ge(setup_pe, 3)
            v.tensor_copy(cc[:, XC:XC + 1], M[:, 0:1]).then_inc(setup_dve, 1)
            dve.wait_ge(setup_pe, 4)
            v.tensor_copy(kc[:], M[0:DK, 0:H]).then_inc(setup_dve, 1)
            dve.wait_ge(setup_pe, 5)
            v.tensor_scalar(rrep[:].rearrange("p (h d) -> p h d", h=H),
                            M[:, 0:H].unsqueeze(2).to_broadcast([P, H, DV]), float(DK) ** -0.5, None, ALU.mult)
            v.tensor_tensor(grep[:].rearrange("p (h d) -> p h d", h=H),
                            M[:, H:2 * H].unsqueeze(2).to_broadcast([P, H, DV]),
                            u[:].unsqueeze(2).to_broadcast([P, H, DV]), ALU.add).then_inc(setup_dve, 1)
            dve.wait_ge(setup_pe, 6)
            v.tensor_scalar(cc[:, BK:BK + 1], M[:, 0:1], 0.5, None, ALU.mult)
            v.tensor_copy(cc[:, LOGIT:LOGIT + 1], M[:, 1:2]).then_inc(setup_dve, 1)
            dve.wait_ge(setup_act, 1)
            link(v.tensor_scalar(cc[:, T1:T1 + 1], cc[:, TCC:TCC + 1], 1.0, None, ALU.add))
            link(v.tensor_tensor(cc[:, CCX:CCX + 1], cc[:, T1:T1 + 1], cc[:, XC:XC + 1], ALU.mult))
            dve.wait_ge(pool_set, 1)
            setup_links = links[0]

            def split(r, s):
                es = r.eslot(s)
                r.wait_read(dve, s)
                r.wait_e(dve, parts_used, s, 2)
                if s[0] == "tanh":
                    v.tensor_copy(eh[:, es, :], e[:, es, :]).then_inc(hi_ready, 1)
                    wait(dve, hi_ready, r.n, N_TANH, s[1] + 1)
                v.tensor_tensor(el[:, es, :], e[:, es, :], eh[:, es, :], ALU.subtract).then_inc(parts_ready, 1)

            def body(r):
                n, m = r.n, r.m
                if n is not None:
                    links[0] = setup_links
                for s in r.steps:
                    per = ATTN_LINKS
                    if s[0] in ELEMENT_KINDS:
                        split(r, s)
                    elif s[0] == "use" and s[1][0] == "relu" and s[1][1] % 2 == 1:
                        ex = s[1][1] // 2
                        r.wait_e(dve, parts_used, s[1])
                        wait(dve, cwb_ready[ex % 2], m, 8 * EX, 16 * (ex // 2 + 1))
                        wait(dve, acc_added, m, EX, ex - 1)
                        v.scalar_tensor_tensor(prod[:, ex % 2, :], Y[:], b2T[:, ex:ex + 1], cwb[:, ex % 2, :],
                                               ALU.add, ALU.mult).then_inc(prod_ready, 1)
                    elif s[0] == "fin":
                        wait(dve, fin_ready, m, 1, 1)
                        wait(dve, out_done, m, 16, 0)
                        v.tensor_tensor(outs[:].rearrange("p t d -> p (t d)"), Y[:],
                                        h2[:].rearrange("p t d -> p (t d)"), ALU.add).then_inc(out_ready, 1)
                    elif s[0] == "proj":
                        b0, b1 = 2 * r.slot(s), 2 * r.slot(s, 1)
                        wait(dve, rounded, n, 3, 1)
                        for a in range(ATT):
                            q = slice(a * ROWS, (a + 1) * ROWS)
                            ins = v.scalar_tensor_tensor(kz[q, a, :], trnd[q, :], con[q, C_MK:C_MK + 1], W[q, b0, :],
                                                         ALU.mult, ALU.add)
                        ins.then_inc(w_read[r.slot(s)], 1)
                        wait(dve, rounded, n, 3, 2)
                        v.scalar_tensor_tensor(qs[:], trnd[:], con[:, C_MQ:C_MQ + 1], M[:], ALU.mult, ALU.add
                                               ).then_inc(m_read, 1)
                        r.wait_full(dve, s, 1)
                        vv = W[:, b1:b1 + 2, :].rearrange("p k (g c) -> p (k g) c", c=C)
                        link(v.tensor_copy(v1h[:, :, 0:C], vv), n, per)
                        v.tensor_tensor(v1l[:, :, 0:C], vv, v1h[:, :, 0:C], ALU.subtract
                                        ).then_inc(w_read[r.slot(s, 1)], 1)
                    elif s[0] == "max":
                        t, pair = divmod(s[1], 2)
                        c0 = pair * 2 * ROWS + SHIFT
                        slot = r.slot(s)
                        r.wait_full(dve, s)
                        v.tensor_reduce(nm[:, t, c0:c0 + ROWS + 1:ROWS], W[:, 2 * slot:2 * slot + 2, :], AX_X, ALU.max,
                                        negate=True).then_inc(w_read[slot], 1)
                    elif s[0] == "shift":
                        lastmax = ("max", N_MAX - 1)
                        r.wait_read(dve, lastmax)
                        r.wait_read(dve, ("max", N_MAX - 2))
                        v.tensor_copy(nm[:, :, SHIFT + 1::ROWS], nm[:, :, SHIFT::ROWS]).then_inc(shift_ready, 1)
                        wait(dve, rounded, n, 3, 3)
                        v.scalar_tensor_tensor(qs[:], trnd[:], con[:, C_MQ:C_MQ + 1], M[:], ALU.mult, ALU.add
                                               ).then_inc(m_read, 1)
                    elif s[0] == "norm":
                        assert r.slot(s) == 0
                        r.wait_full(dve, s, 1)
                        o = W[:, :, 0:ATT * (C + 1)].rearrange("p t (s k c) -> p t s k c", s=2, k=2)
                        den = sm[:, S_DEN:S_DEN + 16].rearrange("p (t s k) -> p t s k", s=2, k=2)
                        link(v.reciprocal(den, o[:, :, :, :, C]), n, per)
                        link(v.tensor_tensor(den[:, :, :, 0], den[:, :, :, 0],
                                             ag[:].unsqueeze(1).to_broadcast([P, LT, 2]), ALU.mult), n, per)
                        hv = h1[:].rearrange("p t (s c) -> p t s c", s=2)
                        xv = x[:].rearrange("p t (s c) -> p t s c", s=2)
                        v.tensor_tensor(xv, o[:, :, :, 0, 0:C], den[:, :, :, 0:1].to_broadcast([P, LT, 2, C]), ALU.mult)
                        ins = v.tensor_tensor(hv, o[:, :, :, 1, 0:C], den[:, :, :, 1:2].to_broadcast([P, LT, 2, C]),
                                              ALU.mult)
                        ins.then_inc(w_read[0], 1)
                        r.wait_read(dve, s)
                        v.tensor_tensor(h1[:], h1[:], x[:], ALU.add).then_inc(w_read[1], 1)
                    elif s[0] == "ln1":
                        r.wait_read(dve, ("norm", 0), 1)
                        ins = layer_norm(lambda t: h1[:, t, :], lambda t: x[:, t, :], LT, n, per, 2,
                                         bn=sm[:, S_BN:], mv=sm[:, S_MV:], ve=sm[:, S_VE:], rs=sm[:, S_RS:],
                                         n_rstd=n, per_rstd=2)
                        ins.then_inc(x_ready, 1)
                        wait(dve, m_read, n, NM, MU["xT"])
                        link(v.tensor_copy(xh[:], xT[:]), n, per)
                        v.tensor_tensor(xl[:], xT[:], xh[:], ALU.subtract).then_inc(xp_ready, 1)
                        link(v.tensor_tensor(sm[:, S_SB:S_SB + 1], sm[:, S_SX:S_SX + 1], cc[:, XC:XC + 1], ALU.add),
                             n, per)
                    elif s[0] == "gates":
                        wait(dve, m_read, n, NM, MU["tk"])
                        v.tensor_scalar(tk[:], tk[:], cc[:, XC:XC + 1], sm[:, S_SB:S_SB + 1], ALU.mult, ALU.add
                                        ).then_inc(ck_ready, 1)
                        wait(dve, m_read, n, NM, MU["tq"])
                        v.tensor_tensor_reduce(out=tq[:], in0=tq[:], in1=xT[:], scale=1.0, scalar=0.0, op0=ALU.mult,
                                               op1=ALU.add, accum_out=sm[:, S_ST:S_ST + 1]).then_inc(chain, 1)
                        links[0] += 1
                        wait(dve, chain, n, per, links[0])
                        dst = colc[:, n:n + 1] if isinstance(n, int) else colc[:, bass.ds(n, 1)]
                        v.tensor_scalar(dst, sm[:, S_ST:S_ST + 1], sm[:, S_SX:S_SX + 1], None, ALU.add)
                    elif s[0] == "g":
                        h = s[1]
                        wait(dve, m_read, n, NM, MU["g"] + h)
                        if h >= 2:
                            r.wait_full(dve, ("tanh", 2 * h - 3))
                        link(v.tensor_copy(gh[:, h % 2, :], gf[:]), n, per)
                        v.tensor_tensor(gl[:, h % 2, :], gf[:], gh[:, h % 2, :], ALU.subtract).then_inc(g_ready, 1)
                    elif s[0] == "mix":
                        wait(dve, m_ready, n, NM, MU["mix"])
                        if m is not None:
                            wait(dve, out_ready, m, 1, 1)
                        v.tensor_tensor(h2[:].rearrange("p t d -> p (t d)"), M[:],
                                        h1[:].rearrange("p t d -> p (t d)"), ALU.add).then_inc(m_read, 1)
                        wait(dve, m_read, n, NM, MU["mix"])
                        wait(dve, vz_ready, n, 1, 1)
                        ins = layer_norm(lambda t: h2[:, t, :], lambda t: x[:, t, :], LT, n, per, 3,
                                         bn=sm[:, S_BN:], mv=sm[:, S_MV:], ve=sm[:, S_VE:], rs=sm[:, S_RS:],
                                         n_rstd=n, per_rstd=2)
                        ins.then_inc(x_ready, 1)
                        wait(dve, m_read, n, NM, MU["yT"])
                        link(v.tensor_copy(yh[:], xT[:]), n, per)
                        v.tensor_tensor(yl[:], xT[:], yh[:], ALU.subtract).then_inc(yp_ready, 1)
                    elif s[0] == "route":
                        wait(dve, m_ready, n, NM, MU["logits"])
                        v.tensor_tensor(rt[:, 0, :, :], M[:, 0:LT * EX].rearrange("p (t e) -> p t e", e=EX),
                                        brb[:].unsqueeze(1).to_broadcast([P, LT, EX]), ALU.add).then_inc(m_read, 1)
                        wait(dve, m_read, n, NM, MU["logits"])
                        top2(P, LT, n, per, ex_ready, n, 1, 1, logits_ready).then_inc(cw_ready, 1)
                if n is not None:
                    assert links[0] - setup_links == ATTN_LINKS, links[0] - setup_links

            rounds(dve, body)

            links[0] = setup_links + B * ATTN_LINKS
            link(v.tensor_scalar(colc[:], colc[:], cc[:, CCX:CCX + 1], 0.5, ALU.add, ALU.mult))
            v.tensor_copy(sm[:, 0:1], con[:, 0:1]).then_inc(tail_cols, 1)
            dve.wait_ge(tail_pe, 1)
            link(v.tensor_tensor(hc, clsr[:], M[0:B, 0:P], ALU.add))
            ins = layer_norm(lambda t: hc, lambda t: clsx[:], 1, 0, 0, 1, rows=B, bn=cc[:, BN:BN + 6],
                             mv=cc[:, MV:MV + 2], ve=cc[:, VAR:VAR + 1], rs=cc[:, RSTD:RSTD + 1],
                             rstd=tail_pool, n_rstd=0)
            ins.then_inc(tail_x, 1)
            dve.wait_ge(tail_pe, 2)
            link(v.tensor_copy(xcT, M[:, 0:B]))
            link(v.tensor_copy(xch, xcT))
            v.tensor_tensor(xcl, xcT, xch, ALU.subtract).then_inc(tail_x, 1)
            dve.wait_ge(tail_pe, 3)
            link(v.tensor_tensor(rt[0:B, 0, 0, :], M[0:B, 0:EX], brb[0:B, :], ALU.add))
            top2(B, 1, 0, 0, tail_act, 0, 0, 1, tail_dve_l).then_inc(tail_dve_w, 1)
            dve.wait_ge(tail_pe, 4)
            v.tensor_copy(cwT[:, 0:B], M[0:EX, 0:B]).then_inc(tail_x, 1)
            dve.wait_ge(tail_pe, 5)
            link(v.tensor_copy(gf[:, 0:EX * FB * B], AC[:, 0, 0:EX * FB * B]))
            link(v.tensor_copy(gh[:, 0, 0:EX * FB * B], gf[:, 0:EX * FB * B]))
            v.tensor_tensor(gl[:, 0, 0:EX * FB * B], gf[:, 0:EX * FB * B], gh[:, 0, 0:EX * FB * B], ALU.subtract
                            ).then_inc(tail_x, 1)
            dve.wait_ge(tail_pe, 6)
            v.tensor_tensor(x[0:B, 3, :], hc, Y[0:B, 0:D], ALU.add).then_inc(tail_dve, 1)

        @block.tensor
        def _(pe):
            mm, tr = nc.tensor.matmul, nc.tensor.transpose
            pe.sem_inc(fin_ready, 1)

            pe.wait_ge(consts_in, 16 * len(SMALL))
            for h in range(H):
                ins = mm(AC[:, h // 4, (h % 4) * P:(h % 4 + 1) * P], wqT[:, h, :], wkT[:, h, :], start=True, stop=True)
            ins.then_inc(setup_pe, 1)
            for h in range(H):
                ins = mm(Y[:, h:h + 1], wkT[:, h, :], biasT[:, h:h + 1], start=True, stop=True)
            ins.then_inc(setup_pe, 1)
            pe.wait_ge(setup_dve, 1)
            mm(M[:, 0:1], clsx[0:1, :], ident[0:1, 0:1], start=True, stop=True).then_inc(setup_pe, 1)
            pe.wait_ge(setup_dve, 3)
            for h in range(H):
                ins = mm(M[0:DK, h:h + 1], xT[:, h * DK:(h + 1) * DK], cc[:, XC:XC + 1], start=True, stop=True)
            ins.then_inc(setup_pe, 1)
            pe.wait_ge(setup_dve, 4)
            for h in range(H):
                mm(M[:, h:h + 1], wqT[:, h, :], kc[:, h:h + 1], start=True, stop=True)
            for h in range(H):
                ins = mm(M[:, H + h:H + h + 1], m32[:, h, :], cc[:, XC:XC + 1], start=True, stop=True)
            ins.then_inc(setup_pe, 1)
            pe.wait_ge(setup_dve, 5)
            mm(M[:, 0:1], urep, cc[:, XC:XC + 1], start=True, stop=True)
            mm(M[:, 1:2], grep[:], cc[:, XC:XC + 1], start=True, stop=True).then_inc(setup_pe, 1)
            pe.wait_ge(setup_dve, 6)

            def three(out, a, b, start, stop):
                mm(out, a[0], b[0], start=start, stop=False)
                mm(out, a[0], b[1], start=False, stop=False)
                return mm(out, a[1], b[0], start=False, stop=stop)

            def tile(t):
                return slice(t * P, (t + 1) * P)

            def use(r, s):
                kind, i = s
                es = r.eslot(s)
                r.wait_e(pe, parts_ready, s)
                if kind == "exp":
                    at, half = divmod(i, 2)
                    if half == 0:
                        wait(pe, ac_read[at % 2], r.n, 3, at // 2)
                    for k in range(2):
                        g, el_ = (2 * half + k) * ATT + at, slice(k * L, (k + 1) * L)
                        ins = three(AC[0:C + 1, at % 2, :], (v1h[:, g, 0:C + 1], v1l[:, g, 0:C + 1]),
                                    (eh[:, es, el_], el[:, es, el_]), half == 0 and k == 0, half == 1 and k == 1)
                elif kind == "tanh":
                    h, half = divmod(i, 2)
                    if h % 4 == 0 and half == 0:
                        wait(pe, ac_read[h // 4], r.n, 3, 2)
                        wait(pe, vz_ready, r.n, 1, 1)
                    for k in range(2):
                        val, el_ = vz[:, 2 * half + k, h, :], slice(k * L, (k + 1) * L)
                        mm(AC[:, h // 4, :], val, eh[:, es, el_], start=h % 4 == 0 and half == 0 and k == 0, stop=False)
                        ins = mm(AC[:, h // 4, :], val, el[:, es, el_], start=False,
                                 stop=h % 4 == 3 and half == 1 and k == 1)
                else:
                    ex, half = divmod(i, 2)
                    if half == 0:
                        wait(pe, prod_ready, r.m, EX, ex)
                        wait(pe, out_ready, r.m, 1, 0)
                    for k in range(2):
                        f, el_ = tile(2 * half + k), slice(k * L, (k + 1) * L)
                        ins = three(Y[:], (w2h[:, ex, f], w2l[:, ex, f]), (eh[:, es, el_], el[:, es, el_]),
                                    half == 0 and k == 0, half == 1 and k == 1)
                ins.then_inc(parts_used, 1)

            def body(r):
                n, m = r.n, r.m
                for s in r.steps:
                    kind, i = s
                    if kind == "use":
                        use(r, i)
                        continue
                    if kind in W_KINDS:
                        r.wait_read(pe, s, before=1)
                        slot = r.slot(s)
                    if kind == "proj":
                        wait(pe, xin_ready, n, 16, 16)
                        mm(W[:, 2 * slot, :], wqk[:, P:2 * P], xin[:], start=True, stop=True).then_inc(w_ready, 1)
                        wait(pe, m_read, n, NM, 0)
                        mm(M[:], wqk[:, 0:P], xin[:], start=True, stop=True).then_inc(m_ready, 1)
                        r.wait_read(pe, s, 1, before=1)
                        for t in range(LT):
                            c0 = (t % 2) * ATT * C
                            ins = mm(W[:, 2 * r.slot(s, 1) + t // 2, c0:c0 + ATT * C], xin[:, tile(t)], wv[:],
                                     start=True, stop=True)
                        ins.then_inc(w_ready, 1)
                    elif kind == "max":
                        t, pair = divmod(i, 2)
                        if i == 0:
                            r.wait_read(pe, ("proj", 0))
                            wait(pe, m_read, n, NM, MU["q"])
                        for k in range(2):
                            ins = mm(W[:, 2 * slot + k, :], qs[:, tile(t)], kz[:, 2 * pair + k, :], start=True, stop=True)
                        ins.then_inc(w_ready, 1)
                    elif kind == "shift":
                        wait(pe, shift_ready, n, 1, 1)
                        for t in range(LT):
                            ins = mm(M[:, tile(t)], nm[:, t, :], ident, start=False, stop=t == LT - 1,
                                     skip_group_check=True)
                        ins.then_inc(m_ready, 1)
                    elif kind == "exp":
                        at, half = divmod(i, 2)
                        if i == 0:
                            wait(pe, m_read, n, NM, MU["qs"])
                            r.wait_read(pe, ("proj", 0), 1)
                        for k in range(2):
                            ins = mm(W[:, 2 * slot + k, :], kz[:, at, tile(2 * half + k)], qs[:], start=True, stop=True)
                        ins.then_inc(w_ready, 1)
                    elif kind == "norm":
                        r.wait_read(pe, s, 1, before=1)
                        for k in range(2):
                            wait(pe, ac_read[k], n, 3, 2)
                        for t in range(LT):
                            for at in range(ATT):
                                ins = tr(W[:, t, at * (C + 1):(at + 1) * (C + 1)], ot[0:C + 1, at, tile(t)],
                                         ident[0:C + 1, 0:C + 1])
                            if t % 2:
                                ins.then_inc(w_ready, 1)
                    elif kind == "ln1":
                        wait(pe, x_ready, n, 2, 1)
                        for t in range(LT):
                            ins = tr(M[:, tile(t)], x[:, t, :], ident)
                        ins.then_inc(m_ready, 1)
                    elif kind == "gates":
                        wait(pe, m_read, n, NM, MU["xT"])
                        mm(M[:], rrep[:], xT[:], start=True, stop=True).then_inc(m_ready, 1)
                        wait(pe, m_read, n, NM, MU["tk"])
                        mm(M[:], grep[:], xT[:], start=True, stop=True).then_inc(m_ready, 1)
                    elif kind == "g":
                        if i == 0:
                            wait(pe, xp_ready, n, 1, 1)
                        wait(pe, m_read, n, NM, MU["g"] + i - 1)
                        three(M[:], (mh[:, i, :], ml[:, i, :]), (xh[:], xl[:]), True, True).then_inc(m_ready, 1)
                    elif kind == "tanh":
                        h, half = divmod(i, 2)
                        wait(pe, g_ready, n, H, h + 1)
                        for k in range(2):
                            t = tile(2 * half + k)
                            ins = three(W[:, 2 * slot + k, :], (xh[:, t], xl[:, t]), (gh[:, h % 2, :], gl[:, h % 2, :]),
                                        True, True)
                        ins.then_inc(w_ready, 1)
                    elif kind == "mix":
                        for k in range(2):
                            wait(pe, ac_read[k], n, 3, 3)
                        wait(pe, ck_ready, n, 1, 1)
                        wait(pe, m_read, n, NM, MU["mix"] - 1)
                        for t in range(LT):
                            mm(M[:, tile(t)], AT[:, 0, tile(t)], con[:, C_SEL:C_SEL + P], start=True, stop=False)
                            mm(M[:, tile(t)], AT[:, 1, tile(t)], con[:, C_SEL + P:C_SEL + 2 * P], start=False, stop=False)
                            ins = mm(M[:, tile(t)], tk[:, tile(t)], con[:, C_HALF:C_HALF + P], start=False, stop=True)
                        ins.then_inc(m_ready, 1)
                        wait(pe, x_ready, n, 2, 2)
                        for t in range(LT):
                            ins = tr(M[:, tile(t)], x[:, t, :], ident)
                        ins.then_inc(m_ready, 1)
                    elif kind == "route":
                        wait(pe, m_read, n, NM, MU["yT"])
                        for t in range(LT):
                            ins = mm(M[:, t * EX:(t + 1) * EX], xT[:, tile(t)], wr[:], start=True, stop=True)
                        ins.then_inc(m_ready, 1)
                        wait(pe, cw_ready, n, 1, 1)
                        for t in range(LT):
                            ins = tr(M[0:EX, tile(t)], rt[:, 0, t, :], ident)
                        ins.then_inc(m_ready, 1)
                    elif kind == "relu":
                        ex, half = divmod(i, 2)
                        if i == 0:
                            wait(pe, yp_ready, m, 1, 1)
                            pe.wait_ge(wts_lo, 2 * EX)
                        for k in range(2):
                            f = tile(2 * half + k)
                            ins = three(W[:, 2 * slot + k, :], (w1h[:, ex, f], w1l[:, ex, f]), (yh[:], yl[:]), True, True)
                        ins.then_inc(w_ready, 1)
                    elif kind == "fin":
                        wait(pe, acc_added, m, EX, EX)
                        for t in range(LT):
                            ins = tr(Y[:, tile(t)], acc[:, tile(t)], ident)
                        ins.then_inc(fin_ready, 1)

            rounds(pe, body)

            def hidden(ex):
                pe.wait_ge(tail_act, ex + 2)
                for f in range(FB):
                    c = (ex * FB + f) * B
                    ins = tr(AC[:, 0, c:c + B], ez[0:B, ex % 4, tile(f)], ident[0:B, 0:B])
                ins.then_inc(tail_t if ex < EX - 1 else tail_pe, 1)

            pe.wait_ge(tail_cols, 1)
            pe.wait_ge(m_read, B * NM)
            tr(M[0:B, 0:P], colc[:], ident).then_inc(tail_pe, 1)
            pe.wait_ge(tail_x, 1)
            tr(M[:, 0:B], clsx[:], ident[0:B, 0:B]).then_inc(tail_pe, 1)
            pe.wait_ge(tail_x, 2)
            mm(M[0:B, 0:EX], xcT, wr[:], start=True, stop=True).then_inc(tail_pe, 1)
            for ex in range(EX):
                if ex == 0:
                    Round(last, None, B - 1, W3, E3, B - 1, NW1, NE1).wait_read(pe, ("relu", N_RELU - 1))
                    Round(last, None, B - 1, W3, E3, B - 1, NW1, NE1).wait_read(pe, ("relu", N_RELU - 2))
                if ex >= 4:
                    pe.wait_ge(tail_act, ex - 2)
                mm(W[0:B, ex % 4, :], con[0:EX, C_HOT + ex * B:C_HOT + (ex + 1) * B], b1e[:], start=True, stop=False)
                three(W[0:B, ex % 4, :], (xch, xcl), (w1h[:, ex, :], w1l[:, ex, :]), False, True).then_inc(tail_z, 1)
                if ex == 0:
                    pe.wait_ge(tail_dve_w, 1)
                    tr(M[0:EX, 0:B], rt[0:B, 0, 0, :], ident[0:B, 0:B]).then_inc(tail_pe, 1)
                if ex >= 2:
                    hidden(ex - 2)
            hidden(EX - 2)
            hidden(EX - 1)
            pe.wait_ge(tail_x, 3)
            mm(Y[0:B, 0:D], cwT[:, 0:B], b2e[:], start=True, stop=False)
            pe.wait_ge(tail_x, 4)
            for c in range(EX * FB):
                hid = slice(c * B, (c + 1) * B)
                w = (w2h[:, c // FB, tile(c % FB)], w2l[:, c // FB, tile(c % FB)])
                ins = three(Y[0:B, 0:D], (gh[:, 0, hid], gl[:, 0, hid]), w, False, c == EX * FB - 1)
            ins.then_inc(tail_pe, 1)


def kernel(**inputs):
    import concourse.bacc as _bacc
    from concourse.bass_utils import run_bass_kernel_spmd as _run

    i = {k: np.asarray(v) for k, v in inputs.items()}
    f4 = np.float32

    def tok(k):
        return i[f"L0_tok_w{k}"]

    wqk, wv = np.zeros((D, 2 * P), f4), np.zeros((D, ATT * C), f4)
    for a, (q, k, v, sq, sk) in enumerate(((1, 2, 3, 0, 0), (4, 5, 6, 0, 1), (7, 8, 9, 1, 1), (10, 11, 12, 1, 0))):
        for rep in range(3):
            c0 = a * ROWS + rep * DQ
            wqk[sq * C:(sq + 1) * C, c0:c0 + DQ] = tok(q)
            wqk[sk * C:(sk + 1) * C, P + c0:P + c0 + DQ] = tok(k)
        wv[sk * C:(sk + 1) * C, a * C:(a + 1) * C] = tok(v)
    xT = i["x"].transpose(0, 3, 2, 1).reshape(B, D, L)
    Wq, Wk = i["L0_attn_Wq"], i["L0_attn_Wk"]
    W1, W2, b1, b2 = i["L0_ffn_W1"], i["L0_ffn_W2"], i["L0_ffn_b1"], i["L0_ffn_b2"]
    arrays = {
        "consts": constants(),
        "wqk": wqk,
        "wv": wv,
        "wqT": Wq.T.reshape(H, DK, D).transpose(1, 0, 2),
        "wkT": Wk.T.reshape(H, DK, D).transpose(1, 0, 2),
        "wk": Wk,
        "wr": i["L0_ffn_Wr"],
        "brb": np.broadcast_to(i["L0_ffn_br"], (P, EX)),
        "ag": np.broadcast_to(np.concatenate([i["L0_tok_alpha"], i["L0_tok_gamma"]]), (P, 2)),
        "b1T": b1.reshape(EX, FB, P).transpose(2, 0, 1).reshape(P, EX * FB),
        "b2T": b2.T,
        "b1": b1,
        "b2": b2,
        "biasT": i["L0_attn_rel_content_bias"].reshape(H, DK).T,
        "cls": np.broadcast_to(i["cls_tok"].reshape(1, D), (B, D)),
        "xT": np.concatenate([xT, xT[-1:]]),
        "w1": W1.transpose(1, 0, 2),
        "w2": W2.reshape(EX, FB, P, D).transpose(2, 0, 1, 3).reshape(P, EX, F),
    }
    arrays = {k: np.ascontiguousarray(a) for k, a in arrays.items()}
    nc = _bacc.Bacc("TRN2", target_bir_lowering=False, num_devices=1)
    A = {k: nc.dram_tensor(f"in_{k}", a.shape, F32, kind="ExternalInput").ap() for k, a in arrays.items()}
    A["out"] = nc.dram_tensor("out_0", (B, L + 1, D), F32, kind="ExternalOutput").ap()
    build(nc, A)
    r = _run(nc, [{f"in_{k}": a for k, a in arrays.items()}], core_ids=[0])
    return r.results[0]["out_0"]
```

```python
from contextlib import ExitStack

import numpy as np

import concourse.bass as bass
from concourse import mybir

B, L, C = 8, 512, 64
D = 2 * C
DQ = C // 8
ATT = 4
H, DK = 8, 64
DV = D // H
EX, F = 8, 512
P = 128
LT = L // P
FB = F // P
LN_EPS = 1e-5

F32 = mybir.dt.float32
F32R = mybir.dt.float32r
U32 = mybir.dt.uint32
ACT = mybir.ActivationFunctionType
ALU = mybir.AluOpType
AX_X = mybir.AxisListType.X

ROWS = 32
SHIFT = 3 * DQ
VW = C + 2

C_ID, C_SEL, C_HALF, C_IOTA = 0, P, 3 * P, 4 * P
C_MQ, C_MK, C_ONE, C_NHALF = C_IOTA + EX, C_IOTA + EX + 1, C_IOTA + EX + 2, C_IOTA + EX + 3
C_HOT = C_NHALF + 1
C_W = C_HOT + EX * B


def constants():
    c = np.zeros((P, C_W), np.float32)
    c[:, C_ID:C_ID + P] = np.eye(P)
    for h in range(H):
        for part in range(2):
            for d in range(DV):
                c[(h % 4) * 2 * DV + part * DV + d, C_SEL + (h // 4) * P + h * DV + d] = 0.5
    c[:, C_HALF:C_HALF + P] = 0.5 * np.eye(P)
    c[:, C_IOTA:C_IOTA + EX] = np.arange(EX)
    for a in range(ATT):
        r = a * ROWS
        c[r + DQ:r + 2 * DQ, C_MQ] = -1.0
        c[r + SHIFT + 1, C_MQ] = -1.0
        c[r + 2 * DQ:r + 3 * DQ, C_MK] = -1.0
        c[r + SHIFT:r + SHIFT + 2, C_MK] = 1.0
        c[r + SHIFT:r + SHIFT + 2, C_ONE] = 1.0
    c[:, C_NHALF] = -0.5
    for e in range(EX):
        c[e, C_HOT + e * B:C_HOT + (e + 1) * B] = 1.0
    return c


N_MAX, N_EXP, N_TANH, N_RELU = 2 * LT, 2 * ATT, 2 * H, 2 * EX
ELEMENT_KINDS = ("exp", "tanh", "relu")
LAG = 2
CHAIN = 26


def one(*kinds):
    return [(k, 0) for k in kinds]


def some(kind, a, b):
    return [(kind, i) for i in range(a, b)]


FIRST_HALF = one("proj") + some("max", 0, N_MAX) + one("shift") + some("exp", 0, N_EXP)
ORDER = (
    some("relu", 0, 2) + one("norm") + some("relu", 2, 3) + one("ln1") + some("relu", 3, 4) + one("xT")
    + some("relu", 4, 5) + one("xp", "tk") + some("relu", 5, 6) + one("tq", "g")
)
for h_ in range(H):
    ORDER += [("g", h_ + 1)] * (h_ + 1 < H) + some("tanh", 2 * h_, 2 * h_ + 1)
    ORDER += some("relu", 6 + 2 * h_, 7 + 2 * h_) if h_ < 5 else []
    ORDER += one("proj") if h_ == 5 else some("max", h_ - 6, h_ - 5) if h_ > 5 else []
    ORDER += some("tanh", 2 * h_ + 1, 2 * h_ + 2)
    ORDER += some("relu", 7 + 2 * h_, 8 + 2 * h_) if h_ < 5 else []
    ORDER += one("fin") if h_ == 6 else []
ORDER += (
    some("max", 2, 3) + one("mix") + some("max", 3, 5) + one("ln2") + some("max", 5, 6) + one("yT")
    + some("max", 6, 7) + one("yp") + some("max", 7, 8) + one("logits") + one("shift") + one("top2")
    + some("exp", 0, 3) + one("cwT") + some("exp", 3, N_EXP)
)
FIRST_KINDS, EXPERT_KINDS = ("proj", "max", "shift", "exp"), ("relu", "fin")
NO_EXPERTS = [s for s in ORDER if s[0] not in EXPERT_KINDS]
NO_FIRST = [s for s in ORDER if s[0] not in FIRST_KINDS]
EXPERTS = [s for s in ORDER if s[0] in EXPERT_KINDS]
assert sorted(FIRST_HALF) == sorted(s for s in ORDER if s[0] in FIRST_KINDS) and len(EXPERTS) == N_RELU + 1


def with_uses(steps, lag):
    out, waiting = [], []
    for s in steps:
        if s[0] in ELEMENT_KINDS:
            out.append(s)
            waiting.append(s)
            if len(waiting) > lag:
                out.append(("use", waiting.pop(0)))
            continue
        needs = {"norm": ("exp",), "mix": ("tanh",), "fin": ("relu",)}.get(s[0], ())
        while any(w[0] in needs for w in waiting):
            out.append(("use", waiting.pop(0)))
        out.append(s)
    return out + [("use", w) for w in waiting]


def build(nc, A):
    with ExitStack() as ctx:
        def sb(name, shape, dt=F32):
            return ctx.enter_context(nc.sbuf_tensor(name, shape, dt))

        def sem(name):
            return ctx.enter_context(nc.semaphore(name))

        con = sb("con", [P, C_W])
        wqk = sb("wqk", [P, 2 * P])
        wv = sb("wv", [P, ATT * C])
        wqT = sb("wqT", [DK, H, P])
        wkT = sb("wkT", [DK, H, P])
        wr = sb("wr", [P, EX])
        brb = sb("brb", [P, EX])
        ag = sb("ag", [P, 2])
        b1T = sb("b1T", [P, EX * FB])
        b2T = sb("b2T", [P, EX])
        b1e = sb("b1e", [EX, F])
        b2e = sb("b2e", [EX, D])
        biasT = sb("biasT", [DK, H])
        clsr = sb("clsr", [B, D])
        clsx = sb("clsx", [B, D])
        w1h, w1l = sb("w1h", [P, EX, F], F32R), sb("w1l", [P, EX, F], F32R)
        w2h, w2l = sb("w2h", [P, EX, F], F32R), sb("w2l", [P, EX, F], F32R)
        mh, ml = sb("mh", [P, H, P], F32R), sb("ml", [P, H, P], F32R)
        u = sb("u", [P, H])
        rrep, grep = sb("rrep", [P, P]), sb("grep", [P, P])
        kc = sb("kc", [DK, H])
        cc = sb("cc", [P, 24])
        xin = sb("xin", [P, L])
        trnd = sb("trnd", [P, L], F32R)
        kz = sb("kz", [P, ATT, L], F32R)
        qs = sb("qs", [P, L], F32R)
        v1h, v1l = sb("v1h", [P, LT * ATT, VW], F32R), sb("v1l", [P, LT * ATT, VW], F32R)
        nm = sb("nm", [P, LT, P])
        e = sb("e", [P, 2, 2 * L])
        eh, el = sb("eh", [P, 2, 2 * L], F32R), sb("el", [P, 2, 2 * L], F32R)
        ot = sb("ot", [P, ATT, L])
        h1, h2 = sb("h1", [P, LT, D]), sb("h2", [P, LT, D])
        x = sb("x", [P, LT, D])
        xT = sb("xT", [P, L])
        xh, xl = sb("xh", [P, L], F32R), sb("xl", [P, L], F32R)
        yh, yl = sb("yh", [P, L], F32R), sb("yl", [P, L], F32R)
        vz = sb("vz", [P, LT, H, P], F32R)
        gf = sb("gf", [P, L])
        gh, gl = sb("gh", [P, 2, L], F32R), sb("gl", [P, 2, L], F32R)
        tk, tq = sb("tk", [P, L]), sb("tq", [P, L])
        sm = sb("sm", [P, 192])
        mx8 = sb("mx8", [P, LT, 8])
        ix8 = sb("ix8", [P, LT, 8], U32)
        rt = sb("rt", [P, 4, LT, EX])
        cwT = sb("cwT", [EX, L])
        mo = sb("mo", [P, 4, L])
        acc = sb("acc", [P, L])
        outs = sb("outs", [P, LT, D])
        colc = sb("colc", [P, B])
        tl = sb("tl", [P, B])
        tr2 = sb("tr2", [P, 2, B], F32R)
        cwd = nc.dram_tensor("cwd", [EX, L], F32).ap()

        W = ctx.enter_context(nc.psum_tensor("W", [P, 4, L], F32))
        AC = ctx.enter_context(nc.psum_tensor("AC", [P, 2, L], F32))
        M = ctx.enter_context(nc.psum_tensor("M", [P, L], F32))
        Y = ctx.enter_context(nc.psum_tensor("Y", [P, L], F32))

        ident = con[:, C_ID:C_ID + P]
        AT = ot[:, 0:2, :]
        cwb, prod = mo[:, 0:2, :], mo[:, 2:4, :]
        ez = e[:].rearrange("p s (k n) -> p (s k) n", k=2)
        hc = x[0:B, 2, :]
        xcT, xch, xcl = tl[:], tr2[:, 0, :], tr2[:, 1, :]
        SMALL = ((con, "consts"), (wqk, "wqk"), (wv, "wv"), (wqT, "wqT"), (wkT, "wkT"), (wr, "wr"), (brb, "brb"),
                 (ag, "ag"), (b1T, "b1T"), (b2T, "b2T"), (b1e, "b1"), (b2e, "b2"), (biasT, "biasT"),
                 (clsr, "cls"), (xT, "wk"))

        consts_in = sem("consts_in")
        wts_in = [sem(f"wts_in{i}") for i in range(4)]
        wts_hi = sem("wts_hi")
        wts_lo = sem("wts_lo")
        pool_set = sem("pool_set")
        setup_pe, setup_dve, setup_act = sem("setup_pe"), sem("setup_dve"), sem("setup_act")
        xin_ready = sem("xin_ready")
        w_ready = sem("w_ready")
        w_read = [sem("w_read0"), sem("w_read1")]
        m_ready = sem("m_ready")
        m_read = sem("m_read")
        ac_read = [sem("ac_read0"), sem("ac_read1")]
        hi_ready = sem("hi_ready")
        parts_ready = sem("parts_ready")
        q_made = sem("q_made")
        q_ready = sem("q_ready")
        v1_hi = sem("v1_hi")
        parts_used = sem("parts_used")
        rounded = sem("rounded")
        shift_ready = sem("shift_ready")
        var_ready = sem("var_ready")
        rstd_ready = sem("rstd_ready")
        x_ready = sem("x_ready")
        vz_hi, vz_ready = sem("vz_hi"), sem("vz_ready")
        xp_ready = sem("xp_ready")
        yp_ready = sem("yp_ready")
        g_ready = sem("g_ready")
        ck_ready = sem("ck_ready")
        logits_ready = sem("logits_ready")
        ex_ready = sem("ex_ready")
        cw_ready = sem("cw_ready")
        cwd_done = sem("cwd_done")
        cwb_ready = [sem("cwb_ready0"), sem("cwb_ready1")]
        prod_ready = sem("prod_ready")
        acc_added = sem("acc_added")
        fin_ready = sem("fin_ready")
        out_ready = sem("out_ready")
        out_done = sem("out_done")
        carried = sem("carried")
        chain = sem("chain")
        tail_pe, tail_act, tail_pool, tail_done = sem("tail_pe"), sem("tail_act"), sem("tail_pool"), sem("tail_done")
        tail_dve, tail_z, tail_t, tail_x = sem("tail_dve"), sem("tail_z"), sem("tail_t"), sem("tail_x")
        tail_dve_l, tail_dve_w, tail_cols = sem("tail_dve_l"), sem("tail_dve_w"), sem("tail_cols")

        credit = [(prod_ready, 2), (acc_added, 2), (out_ready, 1), (fin_ready, 1), (out_done, 16)]

        def wait(eng, s, n, per, k):
            k += sum(c for t, c in credit if t is s)
            if isinstance(n, int):
                if n * per + k > 0:
                    eng.wait_ge(s, n * per + k)
            else:
                eng.wait_ge(s, n * per + k)

        W_KINDS = {"proj": 2, "max": 1, "norm": 2, "exp": 1, "tanh": 1, "relu": 1}
        E_KINDS = {k: 1 for k in ELEMENT_KINDS}

        def positions(steps, takes):
            at, k = {}, 0
            for s in steps:
                if takes.get(s[0], 0):
                    at[s] = k
                    k += takes[s[0]]
            return at, k

        (_, NW), (_, NE) = positions(ORDER, W_KINDS), positions(ORDER, E_KINDS)

        class Round:

            def __init__(self, steps, n, n1, m, full, w0, e0):
                self.steps, self.n, self.n1, self.m = with_uses(steps, LAG), n, n1, m
                (self.w_at, self.w_all), (self.e_at, self.e_all) = positions(steps, W_KINDS), positions(steps, E_KINDS)
                self.full, self.w0, self.e0 = full, w0, e0
                assert w0 % 2 == e0 % 2 == NW % 2 == NE % 2 == 0

            def slot(self, step, j=0):
                return (self.w_at[step] + j) % 2

            def eslot(self, step):
                return self.e_at[step] % 2

            def wait_full(self, eng, step, j=0):
                wait(eng, w_ready, self.full, NW, self.w0 + self.w_at[step] + j + 1)

            def wait_read(self, eng, step, j=0, before=0):
                k = self.w0 + self.w_at[step] + j
                wait(eng, w_read[k % 2], self.full, NW // 2, k // 2 + 1 - before)

            def wait_e(self, eng, s, step, before=0):
                wait(eng, s, self.full, NE, self.e0 + self.e_at[step] + 1 - before)

        r0 = Round(FIRST_HALF, None, 0, None, 0, 0, 0)
        r1 = Round(NO_EXPERTS, 0, 1, None, 0, r0.w_all, r0.e_all)
        W1, E1 = r0.w_all + r1.w_all, r0.e_all + r1.e_all
        LOOP = B - 2
        r8 = Round(NO_FIRST, B - 1, None, B - 2, LOOP, W1, E1)
        r9 = Round(EXPERTS, None, None, B - 1, LOOP, W1 + r8.w_all, E1 + r8.e_all)

        def rounds(eng, body):
            body(r0)
            body(r1)
            with eng.Fori(1, B - 1) as b:
                body(Round(ORDER, b, b + 1, b - 1, b - 1, W1, E1))
            body(r8)
            body(r9)

        def apart(eng):
            eng.sem_inc(carried, 1)

        MU = {"xT": 1, "tk": 2, "tq": 3, "g": 4, "mix": 12, "yT": 13, "logits": 14, "cwT": 15}
        NM = 15
        XC, BK, TCC, CCX, T1, LOGIT = 0, 1, 2, 3, 4, 5
        VAR, RSTD, MV, BN = 8, 9, 10, 12
        S_BN, S_MV, S_VE, S_RS, S_DEN, S_MX, S_SX, S_ST, S_SB, S_R = 0, 24, 32, 36, 48, 64, 80, 81, 82, 96
        nhalf = con[:, C_NHALF:C_NHALF + 1]
        m32 = e[:, 0, :].rearrange("p (h d) -> p h d", h=H)
        urep = e[:, 1, 0:P]

        block = ctx.enter_context(nc.Block())

        @block.sync
        def _(sp):
            sp.sem_inc(out_done, 16)
            for dst, src in SMALL:
                sp.dma_start(dst[:], A[src]).then_inc(consts_in, 16)
            sp.dma_start(xin[:], A["xT"][0]).then_inc(xin_ready, 16)

            def load_weights(c):
                if c >= 4:
                    sp.wait_ge(wts_lo, c - 3)
                if c < 2 * EX:
                    src = A["w1"][:, c, :] if c < EX else A["w2"][:, c - EX, :]
                    sp.dma_start(mo[:, c % 4, :], src).then_inc(wts_in[c % 4], 16)

            for c in range(4):
                load_weights(c)

            def body(r):
                n, n1, m = r.n, r.n1, r.m
                for s in r.steps:
                    if r is r1 and s[0] == "tanh":
                        load_weights(s[1] + 4)
                    if s[0] == "proj":
                        r.wait_full(sp, s, 1)
                        if isinstance(n1, int):
                            sp.dma_start(xin[:], A["xT"][n1 + 1]).then_inc(xin_ready, 16)
                        else:
                            sp.dma_start(xin[:], A["xT"][bass.ds(n1 + 1, 1)].rearrange("a p n -> p (a n)")
                                         ).then_inc(xin_ready, 16)
                    if s[0] == "relu" and s[1] % 2 == 0:
                        ex = s[1] // 2
                        wait(sp, cwd_done, m, 16, 16)
                        apart(sp)
                        wait(sp, prod_ready, m, EX, ex - 1)
                        sp.dma_start(cwb[:, ex % 2, :], cwd[ex:ex + 1, :].partition_broadcast(P)
                                     ).then_inc(cwb_ready[ex % 2], 16)
                    if s[0] == "fin":
                        wait(sp, out_ready, m, 1, 1)
                        if isinstance(m, int):
                            dst = A["out"][m, 1:L + 1, :].rearrange("(t p) d -> p t d", p=P)
                        else:
                            dst = A["out"][bass.ds(m, 1), 1:L + 1, :].rearrange("a (t p) d -> p (a t) d", p=P)
                        sp.dma_start(dst, outs[:]).then_inc(out_done, 16)
                    if s[0] == "cwT":
                        wait(sp, m_read, n, NM, MU["cwT"])
                        if m is not None:
                            for k in range(2):
                                wait(sp, cwb_ready[k], m, 8 * EX, 8 * EX)
                        sp.dma_start(cwd, cwT[:]).then_inc(cwd_done, 16)

            rounds(sp, body)
            sp.wait_ge(tail_dve, 1)
            sp.dma_start(A["out"][:, 0, :], x[0:B, 3, :]).then_inc(tail_done, 16)
            sp.wait_ge(tail_done, 16)
            sp.wait_ge(out_done, 16 * (B + 1))
            sp.wait_ge(xin_ready, 16 * (B + 1))

        @block.gpsimd
        def _(pool):
            g = nc.gpsimd
            pool.sem_inc(acc_added, 2)
            g.memset(nm[:], 0.0)
            g.memset(kz[:].bitcast(F32), 0.0)
            g.memset(v1h[:].bitcast(F32), 1.0)
            g.memset(v1l[:].bitcast(F32), 0.0)
            g.memset(vz[:].bitcast(F32), 0.0).then_inc(pool_set, 1)
            pool.wait_ge(consts_in, 16 * len(SMALL))
            pool.wait_ge(var_ready, 1)
            g.tensor_tensor(cc[0:B, RSTD:RSTD + 1], cc[0:B, VAR:VAR + 1], nhalf[0:B], ALU.pow).then_inc(rstd_ready, 1)

            def split_weights(c):
                pool.wait_ge(wts_hi, c + 1)
                hi, lo = (w1h, w1l) if c < EX else (w2h, w2l)
                g.tensor_tensor(lo[:, c % EX, :], mo[:, c % 4, :], hi[:, c % EX, :], ALU.subtract).then_inc(wts_lo, 1)

            def rstd(n, k):
                wait(pool, var_ready, n, 2, k + 1)
                g.tensor_tensor(sm[:, S_RS:S_RS + LT], sm[:, S_VE:S_VE + LT], nhalf.to_broadcast([P, LT]),
                                ALU.pow).then_inc(rstd_ready, 1)

            def values(n):
                wait(pool, x_ready, n, 2, 1)
                if not isinstance(n, int):
                    wait(pool, m_read, n, NM, 0)
                    apart(pool)
                for lo in range(2):
                    for t in range(LT):
                        xv = x[:, t, :].rearrange("p (k q d) -> p k q d", k=2, q=4)
                        v = vz[:, t, :, :].rearrange("p (k q) c -> p k (q c)", k=2)
                        for q in range(4):
                            at = q * P + q * 2 * DV
                            if lo:
                                ins = g.tensor_tensor(v[:, :, at + DV:at + 2 * DV], xv[:, :, q, :],
                                                      v[:, :, at:at + DV], ALU.subtract)
                            else:
                                ins = g.tensor_copy(v[:, :, at:at + DV], xv[:, :, q, :])
                    if lo:
                        ins.then_inc(vz_ready, 1)
                    else:
                        ins.then_inc(vz_hi, 1)
                        wait(pool, vz_hi, n, 1, 1)

            def body(r):
                for s in r.steps:
                    if r is r1 and s[0] == "tanh":
                        split_weights(s[1])
                    if s[0] == "norm":
                        rstd(r.n, 1)
                    if s[0] == "ln1":
                        values(r.n)
                    if s[0] == "mix":
                        rstd(r.n, 2)
                    if s[0] == "use" and s[1][0] == "relu" and s[1][1] % 2 == 1:
                        ex = s[1][1] // 2
                        wait(pool, prod_ready, r.m, EX, ex + 1)
                        if ex == 0:
                            wait(pool, fin_ready, r.m, 1, 0)
                            apart(pool)
                            g.tensor_copy(acc[:], prod[:, 0, :]).then_inc(acc_added, 1)
                        else:
                            wait(pool, acc_added, r.m, EX, ex)
                            g.tensor_tensor(acc[:], acc[:], prod[:, ex % 2, :], ALU.add).then_inc(acc_added, 1)

            rounds(pool, body)
            wait(pool, var_ready, B, 2, 2)
            g.tensor_tensor(cc[0:B, RSTD:RSTD + 1], cc[0:B, VAR:VAR + 1], nhalf[0:B], ALU.pow).then_inc(tail_pool, 1)

        @block.scalar
        def _(act):
            a = nc.scalar
            act.wait_ge(setup_dve, 6)
            a.activation(cc[:, TCC:TCC + 1], cc[:, LOGIT:LOGIT + 1], ACT.Tanh, scale=0.5).then_inc(setup_act, 1)

            def split_weights(c):
                act.wait_ge(wts_in[c % 4], 16 * (c // 4 + 1))
                a.copy((w1h if c < EX else w2h)[:, c % EX, :], mo[:, c % 4, :]).then_inc(wts_hi, 1)

            def elements(r, s):
                kind, i = s
                slot, es = r.slot(s), r.eslot(s)
                src = W[:, 2 * slot:2 * slot + 2, :]
                dst = e[:, es, :].rearrange("p (k n) -> p k n", k=2)
                dh = eh[:, es, :].rearrange("p (k n) -> p k n", k=2)
                r.wait_full(act, s)
                r.wait_e(act, parts_ready, s, 2)
                if kind == "tanh":
                    a.activation(dst, src, ACT.Tanh, scale=0.5).then_inc(w_read[slot], 1)
                elif kind == "exp":
                    a.activation(dst, src, ACT.Exp, scale=float(DQ) ** -0.5)
                    r.wait_e(act, parts_used, s, 2)
                    a.activation(dh, src, ACT.Exp, scale=float(DQ) ** -0.5).then_inc(w_read[slot], 1)
                else:
                    for k in range(2):
                        a.activation(dst[:, k, :], src[:, k, :], ACT.Relu, bias=b1T[:, 2 * i + k:2 * i + k + 1])
                    r.wait_e(act, parts_used, s, 2)
                    for k in range(2):
                        ins = a.activation(dh[:, k, :], src[:, k, :], ACT.Relu, bias=b1T[:, 2 * i + k:2 * i + k + 1])
                    ins.then_inc(w_read[slot], 1)

            def body(r):
                n, n1 = r.n, r.n1
                for s in r.steps:
                    if r is r1 and s[0] == "tanh":
                        split_weights(s[1])
                    if s[0] in ELEMENT_KINDS:
                        elements(r, s)
                    elif s[0] == "use" and s[1][0] == "exp" and s[1][1] % 2 == 1:
                        at = s[1][1] // 2
                        r.wait_e(act, parts_used, s[1])
                        if at == 0 and n is not None:
                            wait(act, m_ready, n, NM, MU["mix"])
                        a.copy(ot[0:C + 1, at, :], AC[0:C + 1, at % 2, :]).then_inc(ac_read[at % 2], 1)
                    elif s[0] == "use" and s[1][0] == "tanh" and s[1][1] in (H - 1, 2 * H - 1):
                        k = s[1][1] // H
                        r.wait_e(act, parts_used, s[1])
                        a.copy(AT[:, k, :], AC[:, k, :]).then_inc(ac_read[k], 1)
                    elif s[0] == "proj":
                        r.wait_full(act, s)
                        wait(act, q_ready, n1, 2, 0)
                        a.activation(trnd[:], W[:, 2 * r.slot(s), :], ACT.Identity,
                                     bias=con[:, C_ONE:C_ONE + 1]).then_inc(rounded, 1)
                        wait(act, q_made, n1, 2, 1)
                        r.wait_read(act, s)
                        a.copy(trnd[:], AC[:, 0, :]).then_inc(rounded, 1)
                    elif s[0] == "shift":
                        wait(act, q_made, n1, 2, 2)
                        a.copy(trnd[:], AC[:, 0, :]).then_inc(rounded, 1)
                    elif s[0] == "xT":
                        wait(act, m_ready, n, NM, MU["xT"])
                        a.activation(xT[:], M[:], ACT.Identity, accum_out=sm[:, S_SX:S_SX + 1]).then_inc(m_read, 1)
                    elif s[0] == "tk":
                        wait(act, m_ready, n, NM, MU["tk"])
                        a.activation(tk[:], M[:], ACT.Tanh, scale=0.5, bias=cc[:, BK:BK + 1]).then_inc(m_read, 1)
                    elif s[0] == "tq":
                        wait(act, m_ready, n, NM, MU["tq"])
                        a.activation(tq[:], M[:], ACT.Tanh, scale=0.5).then_inc(m_read, 1)
                    elif s[0] == "g":
                        h = s[1]
                        wait(act, m_ready, n, NM, MU["g"] + h)
                        wait(act, g_ready, n, H, h)
                        a.activation(gf[:], M[:], ACT.Identity, bias=u[:, h:h + 1]).then_inc(m_read, 1)
                    elif s[0] == "yT":
                        wait(act, m_ready, n, NM, MU["yT"])
                        a.copy(xT[:], M[:]).then_inc(m_read, 1)
                    elif s[0] == "logits":
                        wait(act, logits_ready, n, 1, 1)
                        a.activation(rt[:, 1, :, :], rt[:, 0, :, :], ACT.Exp).then_inc(ex_ready, 1)
                    elif s[0] == "cwT":
                        wait(act, m_ready, n, NM, MU["cwT"])
                        wait(act, cwd_done, n, 16, 0)
                        a.copy(cwT[:], M[0:EX, :]).then_inc(m_read, 1)

            rounds(act, body)
            act.wait_ge(tail_dve_l, 1)
            a.activation(rt[0:B, 1, 0, :], rt[0:B, 0, 0, :], ACT.Exp).then_inc(tail_act, 1)
            act.wait_ge(tail_dve_w, 1)
            for ex in range(EX):
                act.wait_ge(tail_z, ex + 1)
                if ex >= 4:
                    act.wait_ge(tail_t, ex - 3)
                a.activation(ez[0:B, ex % 4, :], W[0:B, ex % 4, :], ACT.Relu,
                             scale=rt[0:B, 0, 0, ex:ex + 1]).then_inc(tail_act, 1)

        @block.vector
        def _(dve):
            v = nc.vector
            dve.sem_inc(prod_ready, 2)
            dve.sem_inc(out_ready, 1)
            links = [0]

            def link(ins, n=0, per=0):
                links[0] += 1
                ins.then_inc(chain, 1)
                wait(dve, chain, n, per, links[0])

            def moments(src, tiles, rows, bn, mv, ve, n, per):
                for t in range(tiles):
                    ins = v.bn_stats(bn[0:rows, 6 * t:6 * t + 6], src(t))
                link(ins, n, per)
                apart(dve)
                for t in range(tiles):
                    ins = v.bn_aggr(mv[0:rows, 2 * t:2 * t + 2], bn[0:rows, 6 * t:6 * t + 6])
                link(ins, n, per)
                v.tensor_scalar(ve[0:rows, 0:tiles], mv[0:rows, 1:2 * tiles:2], LN_EPS, None, ALU.add
                                ).then_inc(var_ready, 1)

            def normalise(src, dst, tiles, rows, mv, rs):
                for t in range(tiles):
                    ins = v.tensor_scalar(dst(t), src(t), mv[0:rows, 2 * t:2 * t + 1], rs[0:rows, t:t + 1],
                                          ALU.subtract, ALU.mult)
                return ins

            def less_maximum(rows, T, n, per, signal):
                r0_, mxs = rt[0:rows, 0, 0:T, :], sm[0:rows, S_MX:S_MX + T]
                link(v.tensor_reduce(mxs, r0_, AX_X, ALU.max), n, per)
                v.tensor_tensor(r0_, r0_, mxs.unsqueeze(2).to_broadcast([rows, T, EX]), ALU.subtract
                                ).then_inc(signal, 1)

            def top2(rows, T, n, per):
                r0_, r1_, r2_, r3_ = (rt[0:rows, i, 0:T, :] for i in range(4))
                den = sm[0:rows, S_R:S_R + T]
                link(v.tensor_reduce(den, r1_, AX_X, ALU.add), n, per)
                link(v.reciprocal(den, den), n, per)
                link(v.tensor_tensor(r1_, r1_, den.unsqueeze(2).to_broadcast([rows, T, EX]), ALU.mult), n, per)
                apart(dve)
                for t in range(T):
                    ins = v.max(mx8[0:rows, t, :], rt[0:rows, 1, t, :])
                link(ins, n, per)
                apart(dve)
                for t in range(T):
                    ins = v.max_index(ix8[0:rows, t, :], mx8[0:rows, t, :], rt[0:rows, 1, t, :])
                link(ins, n, per)
                iota = con[0:rows, C_IOTA:C_IOTA + EX].unsqueeze(1).to_broadcast([rows, T, EX])
                v.tensor_tensor(r2_, iota, ix8[0:rows, 0:T, 0:1].to_broadcast([rows, T, EX]), ALU.is_equal)
                link(v.tensor_tensor(r3_, iota, ix8[0:rows, 0:T, 1:2].to_broadcast([rows, T, EX]), ALU.is_equal),
                     n, per)
                link(v.tensor_tensor(r2_, r2_, r3_, ALU.add), n, per)
                return v.tensor_tensor(r0_, r2_, r1_, ALU.mult)

            dve.wait_ge(consts_in, 16 * len(SMALL))
            moments(lambda t: clsr[:], 1, B, cc[:, BN:BN + 6], cc[:, MV:MV + 2], cc[:, VAR:VAR + 1], 0, 0)
            dve.wait_ge(rstd_ready, 1)
            normalise(lambda t: clsr[:], lambda t: clsx[:], 1, B, cc[:, MV:MV + 2], cc[:, RSTD:RSTD + 1]
                      ).then_inc(setup_dve, 1)
            dve.wait_ge(setup_pe, 2)
            for k in range(2):
                ins = v.tensor_scalar(m32[:, 4 * k:4 * k + 4, :], AC[:, k, :].rearrange("p (h d) -> p h d", h=4),
                                      float(DK) ** -0.5, None, ALU.mult)
            v.tensor_copy(u[:], Y[:, 0:H])
            link(v.tensor_copy(sm[:, 0:1], con[:, 0:1]))
            v.tensor_copy(urep.rearrange("p (h d) -> p h d", h=H), u[:].unsqueeze(2).to_broadcast([P, H, DV]))
            link(v.tensor_copy(mh[:], m32))
            v.tensor_tensor(ml[:], m32, mh[:], ALU.subtract).then_inc(setup_dve, 1)
            dve.wait_ge(setup_pe, 3)
            v.tensor_copy(cc[:, XC:XC + 1], M[:, 0:1]).then_inc(setup_dve, 1)
            dve.wait_ge(setup_pe, 4)
            v.tensor_copy(kc[:], M[0:DK, 0:H]).then_inc(setup_dve, 1)
            dve.wait_ge(setup_pe, 5)
            v.tensor_scalar(rrep[:].rearrange("p (h d) -> p h d", h=H),
                            M[:, 0:H].unsqueeze(2).to_broadcast([P, H, DV]), float(DK) ** -0.5, None, ALU.mult)
            v.tensor_tensor(grep[:].rearrange("p (h d) -> p h d", h=H),
                            M[:, H:2 * H].unsqueeze(2).to_broadcast([P, H, DV]),
                            u[:].unsqueeze(2).to_broadcast([P, H, DV]), ALU.add).then_inc(setup_dve, 1)
            dve.wait_ge(setup_pe, 6)
            v.tensor_scalar(cc[:, BK:BK + 1], M[:, 0:1], 0.5, None, ALU.mult)
            v.tensor_copy(cc[:, LOGIT:LOGIT + 1], M[:, 1:2]).then_inc(setup_dve, 1)
            dve.wait_ge(setup_act, 1)
            link(v.tensor_scalar(cc[:, T1:T1 + 1], cc[:, TCC:TCC + 1], 1.0, None, ALU.add))
            link(v.tensor_tensor(cc[:, CCX:CCX + 1], cc[:, T1:T1 + 1], cc[:, XC:XC + 1], ALU.mult))
            dve.wait_ge(pool_set, 1)
            setup_links = links[0]

            def split(r, s):
                es = r.eslot(s)
                r.wait_read(dve, s)
                r.wait_e(dve, parts_used, s, 2)
                if s[0] == "tanh":
                    v.tensor_copy(eh[:, es, :], e[:, es, :]).then_inc(hi_ready, 1)
                    wait(dve, hi_ready, r.n, N_TANH, s[1] + 1)
                v.tensor_tensor(el[:, es, :], e[:, es, :], eh[:, es, :], ALU.subtract).then_inc(parts_ready, 1)

            def body(r):
                n, n1, m = r.n, r.n1, r.m
                links[0] = setup_links
                for s in r.steps:
                    per = CHAIN
                    if s[0] in ELEMENT_KINDS:
                        split(r, s)
                    elif s[0] == "use" and s[1][0] == "relu" and s[1][1] % 2 == 1:
                        ex = s[1][1] // 2
                        r.wait_e(dve, parts_used, s[1])
                        wait(dve, cwb_ready[ex % 2], m, 8 * EX, 16 * (ex // 2 + 1))
                        wait(dve, acc_added, m, EX, ex - 1)
                        v.scalar_tensor_tensor(prod[:, ex % 2, :], Y[:], b2T[:, ex:ex + 1], cwb[:, ex % 2, :],
                                               ALU.add, ALU.mult).then_inc(prod_ready, 1)
                    elif s[0] == "fin":
                        wait(dve, fin_ready, m, 1, 1)
                        wait(dve, out_done, m, 16, 0)
                        v.tensor_tensor(outs[:].rearrange("p t d -> p (t d)"), Y[:],
                                        h2[:].rearrange("p t d -> p (t d)"), ALU.add).then_inc(out_ready, 1)
                    elif s[0] == "proj":
                        b0, b1 = 2 * r.slot(s), 2 * r.slot(s, 1)
                        wait(dve, rounded, n1, 3, 1)
                        for a in range(ATT):
                            q = slice(a * ROWS, (a + 1) * ROWS)
                            ins = v.scalar_tensor_tensor(kz[q, a, :], trnd[q, :], con[q, C_MK:C_MK + 1], W[q, b0, :],
                                                         ALU.mult, ALU.add)
                        ins.then_inc(w_read[r.slot(s)], 1)
                        wait(dve, rounded, n1, 3, 2)
                        v.scalar_tensor_tensor(qs[:], trnd[:], con[:, C_MQ:C_MQ + 1], AC[:, 0, :], ALU.mult, ALU.add
                                               ).then_inc(q_ready, 1)
                        r.wait_full(dve, s, 1)
                        vv = W[:, b1:b1 + 2, :].rearrange("p k (g c) -> p (k g) c", c=C)
                        v.tensor_copy(v1h[:, :, 0:C], vv).then_inc(v1_hi, 1)
                        wait(dve, v1_hi, n1, 1, 1)
                        v.tensor_tensor(v1l[:, :, 0:C], vv, v1h[:, :, 0:C], ALU.subtract
                                        ).then_inc(w_read[r.slot(s, 1)], 1)
                    elif s[0] == "max":
                        t, pair = divmod(s[1], 2)
                        c0 = pair * 2 * ROWS + SHIFT
                        slot = r.slot(s)
                        r.wait_full(dve, s)
                        v.tensor_reduce(nm[:, t, c0:c0 + ROWS + 1:ROWS], W[:, 2 * slot:2 * slot + 2, :], AX_X, ALU.max,
                                        negate=True).then_inc(w_read[slot], 1)
                    elif s[0] == "shift":
                        lastmax = ("max", N_MAX - 1)
                        r.wait_read(dve, lastmax)
                        r.wait_read(dve, ("max", N_MAX - 2))
                        v.tensor_copy(nm[:, :, SHIFT + 1::ROWS], nm[:, :, SHIFT::ROWS]).then_inc(shift_ready, 1)
                        wait(dve, rounded, n1, 3, 3)
                        v.scalar_tensor_tensor(qs[:], trnd[:], con[:, C_MQ:C_MQ + 1], AC[:, 0, :], ALU.mult, ALU.add
                                               ).then_inc(q_ready, 1)
                    elif s[0] == "norm":
                        assert r.slot(s) == 0
                        r.wait_full(dve, s, 1)
                        o = W[:, :, 0:ATT * (C + 1)].rearrange("p t (s k c) -> p t s k c", s=2, k=2)
                        den = sm[:, S_DEN:S_DEN + 16].rearrange("p (t s k) -> p t s k", s=2, k=2)
                        link(v.reciprocal(den, o[:, :, :, :, C]), n, per)
                        link(v.tensor_tensor(den[:, :, :, 0], den[:, :, :, 0],
                                             ag[:].unsqueeze(1).to_broadcast([P, LT, 2]), ALU.mult), n, per)
                        hv = h1[:].rearrange("p t (s c) -> p t s c", s=2)
                        xv = x[:].rearrange("p t (s c) -> p t s c", s=2)
                        v.tensor_tensor(xv, o[:, :, :, 0, 0:C], den[:, :, :, 0:1].to_broadcast([P, LT, 2, C]), ALU.mult)
                        ins = v.tensor_tensor(hv, o[:, :, :, 1, 0:C], den[:, :, :, 1:2].to_broadcast([P, LT, 2, C]),
                                              ALU.mult)
                        ins.then_inc(w_read[0], 1)
                        r.wait_read(dve, s)
                        v.tensor_tensor(h1[:], h1[:], x[:], ALU.add).then_inc(w_read[1], 1)
                        r.wait_read(dve, s, 1)
                        moments(lambda t: h1[:, t, :], LT, P, sm[:, S_BN:], sm[:, S_MV:], sm[:, S_VE:], n, per)
                    elif s[0] == "ln1":
                        wait(dve, rstd_ready, n, 2, 2)
                        normalise(lambda t: h1[:, t, :], lambda t: x[:, t, :], LT, P, sm[:, S_MV:], sm[:, S_RS:]
                                  ).then_inc(x_ready, 1)
                    elif s[0] == "xp":
                        wait(dve, m_read, n, NM, MU["xT"])
                        link(v.tensor_copy(xh[:], xT[:]), n, per)
                        v.tensor_tensor(xl[:], xT[:], xh[:], ALU.subtract).then_inc(xp_ready, 1)
                        link(v.tensor_tensor(sm[:, S_SB:S_SB + 1], sm[:, S_SX:S_SX + 1], cc[:, XC:XC + 1], ALU.add),
                             n, per)
                    elif s[0] == "tk":
                        wait(dve, m_read, n, NM, MU["tk"])
                        v.tensor_scalar(tk[:], tk[:], cc[:, XC:XC + 1], sm[:, S_SB:S_SB + 1], ALU.mult, ALU.add
                                        ).then_inc(ck_ready, 1)
                    elif s[0] == "tq":
                        wait(dve, m_read, n, NM, MU["tq"])
                        v.tensor_tensor_reduce(out=tq[:], in0=tq[:], in1=xT[:], scale=1.0, scalar=0.0, op0=ALU.mult,
                                               op1=ALU.add, accum_out=sm[:, S_ST:S_ST + 1]).then_inc(chain, 1)
                        links[0] += 1
                        wait(dve, chain, n, per, links[0])
                        dst = colc[:, n:n + 1] if isinstance(n, int) else colc[:, bass.ds(n, 1)]
                        v.tensor_scalar(dst, sm[:, S_ST:S_ST + 1], sm[:, S_SX:S_SX + 1], None, ALU.add)
                    elif s[0] == "g":
                        h = s[1]
                        wait(dve, m_read, n, NM, MU["g"] + h)
                        if h >= 2:
                            r.wait_full(dve, ("tanh", 2 * h - 3))
                        link(v.tensor_copy(gh[:, h % 2, :], gf[:]), n, per)
                        v.tensor_tensor(gl[:, h % 2, :], gf[:], gh[:, h % 2, :], ALU.subtract).then_inc(g_ready, 1)
                    elif s[0] == "mix":
                        wait(dve, m_ready, n, NM, MU["mix"])
                        if m is not None:
                            wait(dve, out_ready, m, 1, 1)
                        v.tensor_tensor(h2[:].rearrange("p t d -> p (t d)"), M[:],
                                        h1[:].rearrange("p t d -> p (t d)"), ALU.add).then_inc(m_read, 1)
                        wait(dve, m_read, n, NM, MU["mix"])
                        moments(lambda t: h2[:, t, :], LT, P, sm[:, S_BN:], sm[:, S_MV:], sm[:, S_VE:], n, per)
                    elif s[0] == "ln2":
                        wait(dve, rstd_ready, n, 2, 3)
                        wait(dve, vz_ready, n, 1, 1)
                        normalise(lambda t: h2[:, t, :], lambda t: x[:, t, :], LT, P, sm[:, S_MV:], sm[:, S_RS:]
                                  ).then_inc(x_ready, 1)
                    elif s[0] == "yp":
                        wait(dve, m_read, n, NM, MU["yT"])
                        link(v.tensor_copy(yh[:], xT[:]), n, per)
                        v.tensor_tensor(yl[:], xT[:], yh[:], ALU.subtract).then_inc(yp_ready, 1)
                    elif s[0] == "logits":
                        wait(dve, m_ready, n, NM, MU["logits"])
                        v.tensor_tensor(rt[:, 0, :, :], M[:, 0:LT * EX].rearrange("p (t e) -> p t e", e=EX),
                                        brb[:].unsqueeze(1).to_broadcast([P, LT, EX]), ALU.add).then_inc(m_read, 1)
                        wait(dve, m_read, n, NM, MU["logits"])
                        less_maximum(P, LT, n, per, logits_ready)
                    elif s[0] == "top2":
                        wait(dve, ex_ready, n, 1, 1)
                        top2(P, LT, n, per).then_inc(cw_ready, 1)
                if n is not None:
                    assert links[0] - setup_links == CHAIN, links[0] - setup_links

            rounds(dve, body)

            links[0] = setup_links + B * CHAIN
            link(v.tensor_scalar(colc[:], colc[:], cc[:, CCX:CCX + 1], 0.5, ALU.add, ALU.mult))
            v.tensor_copy(sm[:, 0:1], con[:, 0:1]).then_inc(tail_cols, 1)
            dve.wait_ge(tail_pe, 1)
            link(v.tensor_tensor(hc, clsr[:], M[0:B, 0:P], ALU.add))
            moments(lambda t: hc, 1, B, cc[:, BN:BN + 6], cc[:, MV:MV + 2], cc[:, VAR:VAR + 1], 0, 0)
            dve.wait_ge(tail_pool, 1)
            normalise(lambda t: hc, lambda t: clsx[:], 1, B, cc[:, MV:MV + 2], cc[:, RSTD:RSTD + 1]
                      ).then_inc(tail_x, 1)
            dve.wait_ge(tail_pe, 2)
            link(v.tensor_copy(xcT, M[:, 0:B]))
            link(v.tensor_copy(xch, xcT))
            v.tensor_tensor(xcl, xcT, xch, ALU.subtract).then_inc(tail_x, 1)
            dve.wait_ge(tail_pe, 3)
            link(v.tensor_tensor(rt[0:B, 0, 0, :], M[0:B, 0:EX], brb[0:B, :], ALU.add))
            less_maximum(B, 1, 0, 0, tail_dve_l)
            dve.wait_ge(tail_act, 1)
            top2(B, 1, 0, 0).then_inc(tail_dve_w, 1)
            dve.wait_ge(tail_pe, 4)
            v.tensor_copy(cwT[:, 0:B], M[0:EX, 0:B]).then_inc(tail_x, 1)
            dve.wait_ge(tail_pe, 5)
            link(v.tensor_copy(gf[:, 0:EX * FB * B], AC[:, 0, 0:EX * FB * B]))
            link(v.tensor_copy(gh[:, 0, 0:EX * FB * B], gf[:, 0:EX * FB * B]))
            v.tensor_tensor(gl[:, 0, 0:EX * FB * B], gf[:, 0:EX * FB * B], gh[:, 0, 0:EX * FB * B], ALU.subtract
                            ).then_inc(tail_x, 1)
            dve.wait_ge(tail_pe, 6)
            v.tensor_tensor(x[0:B, 3, :], hc, Y[0:B, 0:D], ALU.add).then_inc(tail_dve, 1)

        @block.tensor
        def _(pe):
            mm, tr = nc.tensor.matmul, nc.tensor.transpose
            pe.sem_inc(fin_ready, 1)

            pe.wait_ge(consts_in, 16 * len(SMALL))
            for h in range(H):
                ins = mm(AC[:, h // 4, (h % 4) * P:(h % 4 + 1) * P], wqT[:, h, :], wkT[:, h, :], start=True, stop=True)
            ins.then_inc(setup_pe, 1)
            for h in range(H):
                ins = mm(Y[:, h:h + 1], wkT[:, h, :], biasT[:, h:h + 1], start=True, stop=True)
            ins.then_inc(setup_pe, 1)
            pe.wait_ge(setup_dve, 1)
            mm(M[:, 0:1], clsx[0:1, :], ident[0:1, 0:1], start=True, stop=True).then_inc(setup_pe, 1)
            pe.wait_ge(setup_dve, 3)
            for h in range(H):
                ins = mm(M[0:DK, h:h + 1], xT[:, h * DK:(h + 1) * DK], cc[:, XC:XC + 1], start=True, stop=True)
            ins.then_inc(setup_pe, 1)
            pe.wait_ge(setup_dve, 4)
            for h in range(H):
                mm(M[:, h:h + 1], wqT[:, h, :], kc[:, h:h + 1], start=True, stop=True)
            for h in range(H):
                ins = mm(M[:, H + h:H + h + 1], m32[:, h, :], cc[:, XC:XC + 1], start=True, stop=True)
            ins.then_inc(setup_pe, 1)
            pe.wait_ge(setup_dve, 5)
            mm(M[:, 0:1], urep, cc[:, XC:XC + 1], start=True, stop=True)
            mm(M[:, 1:2], grep[:], cc[:, XC:XC + 1], start=True, stop=True).then_inc(setup_pe, 1)
            pe.wait_ge(setup_dve, 6)

            def three(out, a, b, start, stop):
                mm(out, a[0], b[0], start=start, stop=False)
                mm(out, a[0], b[1], start=False, stop=False)
                return mm(out, a[1], b[0], start=False, stop=stop)

            def tile(t):
                return slice(t * P, (t + 1) * P)

            def use(r, s):
                kind, i = s
                es = r.eslot(s)
                r.wait_e(pe, parts_ready, s)
                if kind == "exp":
                    at, half = divmod(i, 2)
                    if half == 0:
                        wait(pe, ac_read[at % 2], r.n1, 3, at // 2)
                    for k in range(2):
                        g, el_ = (2 * half + k) * ATT + at, slice(k * L, (k + 1) * L)
                        ins = three(AC[0:C + 1, at % 2, :], (v1h[:, g, 0:C + 1], v1l[:, g, 0:C + 1]),
                                    (eh[:, es, el_], el[:, es, el_]), half == 0 and k == 0, half == 1 and k == 1)
                elif kind == "tanh":
                    h, half = divmod(i, 2)
                    if h % 4 == 0 and half == 0:
                        wait(pe, ac_read[h // 4], r.n, 3, 2)
                        wait(pe, vz_ready, r.n, 1, 1)
                    for k in range(2):
                        val, el_ = vz[:, 2 * half + k, h, :], slice(k * L, (k + 1) * L)
                        mm(AC[:, h // 4, :], val, eh[:, es, el_], start=h % 4 == 0 and half == 0 and k == 0, stop=False)
                        ins = mm(AC[:, h // 4, :], val, el[:, es, el_], start=False,
                                 stop=h % 4 == 3 and half == 1 and k == 1)
                else:
                    ex, half = divmod(i, 2)
                    if half == 0:
                        wait(pe, prod_ready, r.m, EX, ex)
                        wait(pe, out_ready, r.m, 1, 0)
                    for k in range(2):
                        f, el_ = tile(2 * half + k), slice(k * L, (k + 1) * L)
                        ins = three(Y[:], (w2h[:, ex, f], w2l[:, ex, f]), (eh[:, es, el_], el[:, es, el_]),
                                    half == 0 and k == 0, half == 1 and k == 1)
                ins.then_inc(parts_used, 1)

            def body(r):
                n, n1, m = r.n, r.n1, r.m
                for s in r.steps:
                    kind, i = s
                    if kind == "use":
                        use(r, i)
                        continue
                    if kind in W_KINDS:
                        r.wait_read(pe, s, before=1)
                        slot = r.slot(s)
                    if kind == "proj":
                        wait(pe, xin_ready, n1, 16, 16)
                        mm(W[:, 2 * slot, :], wqk[:, P:2 * P], xin[:], start=True, stop=True).then_inc(w_ready, 1)
                        wait(pe, ac_read[0], n1, 3, 0)
                        mm(AC[:, 0, :], wqk[:, 0:P], xin[:], start=True, stop=True).then_inc(q_made, 1)
                        r.wait_read(pe, s, 1, before=1)
                        for t in range(LT):
                            c0 = (t % 2) * ATT * C
                            ins = mm(W[:, 2 * r.slot(s, 1) + t // 2, c0:c0 + ATT * C], xin[:, tile(t)], wv[:],
                                     start=True, stop=True)
                        ins.then_inc(w_ready, 1)
                    elif kind == "max":
                        t, pair = divmod(i, 2)
                        if i == 0:
                            r.wait_read(pe, ("proj", 0))
                            wait(pe, q_ready, n1, 2, 1)
                        for k in range(2):
                            ins = mm(W[:, 2 * slot + k, :], qs[:, tile(t)], kz[:, 2 * pair + k, :], start=True, stop=True)
                        ins.then_inc(w_ready, 1)
                    elif kind == "shift":
                        wait(pe, shift_ready, n1, 1, 1)
                        for t in range(LT):
                            ins = mm(AC[:, 0, tile(t)], nm[:, t, :], ident, start=False, stop=t == LT - 1,
                                     skip_group_check=True)
                        ins.then_inc(q_made, 1)
                    elif kind == "exp":
                        at, half = divmod(i, 2)
                        if i == 0:
                            wait(pe, q_ready, n1, 2, 2)
                            r.wait_read(pe, ("proj", 0), 1)
                        for k in range(2):
                            ins = mm(W[:, 2 * slot + k, :], kz[:, at, tile(2 * half + k)], qs[:], start=True, stop=True)
                        ins.then_inc(w_ready, 1)
                    elif kind == "norm":
                        r.wait_read(pe, s, 1, before=1)
                        for k in range(2):
                            wait(pe, ac_read[k], n, 3, 2)
                        for t in range(LT):
                            for at in range(ATT):
                                ins = tr(W[:, t, at * (C + 1):(at + 1) * (C + 1)], ot[0:C + 1, at, tile(t)],
                                         ident[0:C + 1, 0:C + 1])
                            if t % 2:
                                ins.then_inc(w_ready, 1)
                    elif kind == "xT":
                        wait(pe, m_read, n, NM, 0)
                        wait(pe, x_ready, n, 2, 1)
                        for t in range(LT):
                            ins = tr(M[:, tile(t)], x[:, t, :], ident)
                        ins.then_inc(m_ready, 1)
                    elif kind == "tk":
                        wait(pe, m_read, n, NM, MU["xT"])
                        mm(M[:], rrep[:], xT[:], start=True, stop=True).then_inc(m_ready, 1)
                    elif kind == "tq":
                        wait(pe, m_read, n, NM, MU["tk"])
                        mm(M[:], grep[:], xT[:], start=True, stop=True).then_inc(m_ready, 1)
                    elif kind == "g":
                        if i == 0:
                            wait(pe, xp_ready, n, 1, 1)
                        wait(pe, m_read, n, NM, MU["g"] + i - 1)
                        three(M[:], (mh[:, i, :], ml[:, i, :]), (xh[:], xl[:]), True, True).then_inc(m_ready, 1)
                    elif kind == "tanh":
                        h, half = divmod(i, 2)
                        wait(pe, g_ready, n, H, h + 1)
                        for k in range(2):
                            t = tile(2 * half + k)
                            ins = three(W[:, 2 * slot + k, :], (xh[:, t], xl[:, t]), (gh[:, h % 2, :], gl[:, h % 2, :]),
                                        True, True)
                        ins.then_inc(w_ready, 1)
                    elif kind == "mix":
                        for k in range(2):
                            wait(pe, ac_read[k], n, 3, 3)
                        wait(pe, ck_ready, n, 1, 1)
                        wait(pe, m_read, n, NM, MU["mix"] - 1)
                        for t in range(LT):
                            mm(M[:, tile(t)], AT[:, 0, tile(t)], con[:, C_SEL:C_SEL + P], start=True, stop=False)
                            mm(M[:, tile(t)], AT[:, 1, tile(t)], con[:, C_SEL + P:C_SEL + 2 * P], start=False, stop=False)
                            ins = mm(M[:, tile(t)], tk[:, tile(t)], con[:, C_HALF:C_HALF + P], start=False, stop=True)
                        ins.then_inc(m_ready, 1)
                    elif kind == "yT":
                        wait(pe, x_ready, n, 2, 2)
                        for t in range(LT):
                            ins = tr(M[:, tile(t)], x[:, t, :], ident)
                        ins.then_inc(m_ready, 1)
                    elif kind == "logits":
                        wait(pe, m_read, n, NM, MU["yT"])
                        for t in range(LT):
                            ins = mm(M[:, t * EX:(t + 1) * EX], xT[:, tile(t)], wr[:], start=True, stop=True)
                        ins.then_inc(m_ready, 1)
                    elif kind == "cwT":
                        wait(pe, cw_ready, n, 1, 1)
                        for t in range(LT):
                            ins = tr(M[0:EX, tile(t)], rt[:, 0, t, :], ident)
                        ins.then_inc(m_ready, 1)
                    elif kind == "relu":
                        ex, half = divmod(i, 2)
                        if i == 0:
                            wait(pe, yp_ready, m, 1, 1)
                            pe.wait_ge(wts_lo, 2 * EX)
                        for k in range(2):
                            f = tile(2 * half + k)
                            ins = three(W[:, 2 * slot + k, :], (w1h[:, ex, f], w1l[:, ex, f]), (yh[:], yl[:]), True, True)
                        ins.then_inc(w_ready, 1)
                    elif kind == "fin":
                        wait(pe, acc_added, m, EX, EX)
                        for t in range(LT):
                            ins = tr(Y[:, tile(t)], acc[:, tile(t)], ident)
                        ins.then_inc(fin_ready, 1)

            rounds(pe, body)

            def hidden(ex):
                pe.wait_ge(tail_act, ex + 2)
                for f in range(FB):
                    c = (ex * FB + f) * B
                    ins = tr(AC[:, 0, c:c + B], ez[0:B, ex % 4, tile(f)], ident[0:B, 0:B])
                ins.then_inc(tail_t if ex < EX - 1 else tail_pe, 1)

            pe.wait_ge(tail_cols, 1)
            pe.wait_ge(m_read, B * NM)
            tr(M[0:B, 0:P], colc[:], ident).then_inc(tail_pe, 1)
            pe.wait_ge(tail_x, 1)
            tr(M[:, 0:B], clsx[:], ident[0:B, 0:B]).then_inc(tail_pe, 1)
            pe.wait_ge(tail_x, 2)
            mm(M[0:B, 0:EX], xcT, wr[:], start=True, stop=True).then_inc(tail_pe, 1)
            for ex in range(EX):
                if ex == 0:
                    r9.wait_read(pe, ("relu", N_RELU - 1))
                    r9.wait_read(pe, ("relu", N_RELU - 2))
                if ex >= 4:
                    pe.wait_ge(tail_act, ex - 2)
                mm(W[0:B, ex % 4, :], con[0:EX, C_HOT + ex * B:C_HOT + (ex + 1) * B], b1e[:], start=True, stop=False)
                three(W[0:B, ex % 4, :], (xch, xcl), (w1h[:, ex, :], w1l[:, ex, :]), False, True).then_inc(tail_z, 1)
                if ex == 0:
                    pe.wait_ge(tail_dve_w, 1)
                    tr(M[0:EX, 0:B], rt[0:B, 0, 0, :], ident[0:B, 0:B]).then_inc(tail_pe, 1)
                if ex >= 2:
                    hidden(ex - 2)
            hidden(EX - 2)
            hidden(EX - 1)
            pe.wait_ge(tail_x, 3)
            mm(Y[0:B, 0:D], cwT[:, 0:B], b2e[:], start=True, stop=False)
            pe.wait_ge(tail_x, 4)
            for c in range(EX * FB):
                hid = slice(c * B, (c + 1) * B)
                w = (w2h[:, c // FB, tile(c % FB)], w2l[:, c // FB, tile(c % FB)])
                ins = three(Y[0:B, 0:D], (gh[:, 0, hid], gl[:, 0, hid]), w, False, c == EX * FB - 1)
            ins.then_inc(tail_pe, 1)


def kernel(**inputs):
    import concourse.bacc as _bacc
    from concourse.bass_utils import run_bass_kernel_spmd as _run

    i = {k: np.asarray(v) for k, v in inputs.items()}
    f4 = np.float32

    def tok(k):
        return i[f"L0_tok_w{k}"]

    wqk, wv = np.zeros((D, 2 * P), f4), np.zeros((D, ATT * C), f4)
    for a, (q, k, v, sq, sk) in enumerate(((1, 2, 3, 0, 0), (4, 5, 6, 0, 1), (7, 8, 9, 1, 1), (10, 11, 12, 1, 0))):
        for rep in range(3):
            c0 = a * ROWS + rep * DQ
            wqk[sq * C:(sq + 1) * C, c0:c0 + DQ] = tok(q)
            wqk[sk * C:(sk + 1) * C, P + c0:P + c0 + DQ] = tok(k)
        wv[sk * C:(sk + 1) * C, a * C:(a + 1) * C] = tok(v)
    xT = i["x"].transpose(0, 3, 2, 1).reshape(B, D, L)
    Wq, Wk = i["L0_attn_Wq"], i["L0_attn_Wk"]
    W1, W2, b1, b2 = i["L0_ffn_W1"], i["L0_ffn_W2"], i["L0_ffn_b1"], i["L0_ffn_b2"]
    arrays = {
        "consts": constants(),
        "wqk": wqk,
        "wv": wv,
        "wqT": Wq.T.reshape(H, DK, D).transpose(1, 0, 2),
        "wkT": Wk.T.reshape(H, DK, D).transpose(1, 0, 2),
        "wk": Wk,
        "wr": i["L0_ffn_Wr"],
        "brb": np.broadcast_to(i["L0_ffn_br"], (P, EX)),
        "ag": np.broadcast_to(np.concatenate([i["L0_tok_alpha"], i["L0_tok_gamma"]]), (P, 2)),
        "b1T": b1.reshape(EX, FB, P).transpose(2, 0, 1).reshape(P, EX * FB),
        "b2T": b2.T,
        "b1": b1,
        "b2": b2,
        "biasT": i["L0_attn_rel_content_bias"].reshape(H, DK).T,
        "cls": np.broadcast_to(i["cls_tok"].reshape(1, D), (B, D)),
        "xT": np.concatenate([xT, xT[-1:]]),
        "w1": W1.transpose(1, 0, 2),
        "w2": W2.reshape(EX, FB, P, D).transpose(2, 0, 1, 3).reshape(P, EX, F),
    }
    arrays = {k: np.ascontiguousarray(a) for k, a in arrays.items()}
    nc = _bacc.Bacc("TRN2", target_bir_lowering=False, num_devices=1)
    A = {k: nc.dram_tensor(f"in_{k}", a.shape, F32, kind="ExternalInput").ap() for k, a in arrays.items()}
    A["out"] = nc.dram_tensor("out_0", (B, L + 1, D), F32, kind="ExternalOutput").ap()
    build(nc, A)
    r = _run(nc, [{f"in_{k}": a for k, a in arrays.items()}], core_ids=[0])
    return r.results[0]["out_0"]
```

```python
from contextlib import ExitStack

import numpy as np

import concourse.bass as bass
from concourse import mybir

B, L, C = 8, 512, 64
D = 2 * C
DQ = C // 8
ATT = 4
H, DK = 8, 64
DV = D // H
EX, F = 8, 512
P = 128
LT = L // P
FB = F // P
LN_EPS = 1e-5

F32 = mybir.dt.float32
F32R = mybir.dt.float32r
U32 = mybir.dt.uint32
ACT = mybir.ActivationFunctionType
ALU = mybir.AluOpType
AX_X = mybir.AxisListType.X

ROWS = 32
SHIFT = 3 * DQ
VW = C + 2

C_ID, C_SEL, C_HALF, C_IOTA = 0, P, 3 * P, 4 * P
C_MQ, C_MK, C_ONE, C_NHALF = C_IOTA + EX, C_IOTA + EX + 1, C_IOTA + EX + 2, C_IOTA + EX + 3
C_OWN = C_NHALF + 1
C_ONES = C_OWN + ATT
C_PAIR = C_ONES + P
C_W = C_PAIR + EX * B


def constants():
    c = np.zeros((P, C_W), np.float32)
    c[:, C_ID:C_ID + P] = np.eye(P)
    for h in range(H):
        for part in range(2):
            for d in range(DV):
                c[(h % 4) * 2 * DV + part * DV + d, C_SEL + (h // 4) * P + h * DV + d] = 0.5
    c[:, C_HALF:C_HALF + P] = 0.5 * np.eye(P)
    c[:, C_IOTA:C_IOTA + EX] = np.arange(EX)
    for a in range(ATT):
        r = a * ROWS
        c[r:r + ROWS, C_OWN + a] = 1.0
        c[r + DQ:r + 2 * DQ, C_MQ] = -1.0
        c[r + SHIFT + 1, C_MQ] = -1.0
        c[r + 2 * DQ:r + 3 * DQ, C_MK] = -1.0
        c[r + SHIFT:r + SHIFT + 2, C_MK] = 1.0
        c[r + SHIFT:r + SHIFT + 2, C_ONE] = 1.0
    c[:, C_NHALF] = -0.5
    c[:, C_ONES:C_ONES + P] = 1.0
    for e in range(EX):
        for part in range(2):
            for b in range(B):
                c[(2 * e + part) * B + b, C_PAIR + e * B + b] = 1.0
    return c


ELEMENT_KINDS = ("exp", "tanh", "relu")
RING = 4
LAG = 4
CHAIN = 36
LATE = 8


def parse(text):
    steps = []
    for w in text.split():
        k = w.rstrip("0123456789") if w not in ("ln1", "ln2", "top2") else w
        steps.append((k, int(w[len(k):] or 0)))
    return steps


FIRST_HALF = parse("""
    k q v0 setup0 v1 max0 max1 max2 max3 max4 max5 max6 max7 setup1 max8 max9 max10 max11 max12 max13 max14
    max15 setup2 neg shift qshift exp0 exp1 exp2 exp3 setup3 exp4 exp5 exp6 exp7 setup4 exp8 exp9 exp10 exp11
    setup5 exp12 exp13 exp14 exp15
""")
ORDER = parse("""
    norm0 relu8 norm1 relu9 norm2 relu10 relu11 norm3 relu12 relu13 ln1 relu14 relu15 xT xp k relu16 relu17
    relu18 q tk relu19 tq v0 g0 relu20 relu21 relu22 relu23 v1 g1 tanh0 max0 tanh1 tanh2 max1 tanh3 max2 g2
    tanh4 max3 tanh5 tanh6 g3 tanh7 max4 tanh8 tanh9 tanh10 tanh11 max5 tanh12 tanh13 g4 relu24 max6 max7
    tanh14 tanh15 g5 relu25 max8 tanh16 relu26 tanh17 tanh18 max9 tanh19 g6 relu27 max10 tanh20 relu28 tanh21
    tanh22 max11 tanh23 g7 tanh24 max12 max13 tanh25 relu29 tanh26 tanh27 max14 tanh28 relu30 relu31 max15
    tanh29 neg tanh30 tanh31 shift qshift mix mid exp0 fin out exp1 exp2 ln2 exp3 exp4 exp5 exp6 yT yp exp7
    exp8 logits top2 exp9 exp10 exp11 exp12 relu0 relu1 relu2 cwT exp13 relu3 exp14 exp15 relu4 relu5 relu6
    relu7
""")
FIRST_KINDS, EXPERT_KINDS = ("k", "q", "v", "max", "neg", "shift", "qshift", "exp"), ("relu", "fin", "out")


def early(s):
    return s[0] in ("fin", "out") or s[0] == "relu" and s[1] >= LATE


NO_EARLY = [s for s in ORDER if not early(s)]
NO_FIRST = [s for s in ORDER if s[0] not in FIRST_KINDS]
EARLY = [s for s in ORDER if early(s)]
LAST = parse("""
    relu8 cls0 relu9 relu10 relu11 clp0 cls1 relu12 cls2 relu13 relu14 clp2 cls3 relu15 relu16 relu17 clp3 cls4
    relu18 relu19 relu20 clp4 cls5 relu21 relu22 relu23 clp5 cls6 relu24 relu25 relu26 relu27 clp6 cls7 relu28
    relu29 relu30 relu31 fin out
""")
assert [s for s in LAST if s[0] in EXPERT_KINDS] == EARLY
assert sorted(s for s in FIRST_HALF if s[0] != "setup") == sorted(s for s in ORDER if s[0] in FIRST_KINDS)
assert 2 * EX * B <= P and len(ORDER) == len(set(ORDER)) and sum(s[0] in EXPERT_KINDS for s in ORDER) == EX * FB + 2


def with_uses(before, steps, last):
    out, waiting, full = [], [("use", s, True) for s in [s for s in before if s[0] in ELEMENT_KINDS][-LAG:]], []

    def use():
        nonlocal full
        u = waiting.pop(0)
        out.extend(full + [u])
        kind, i = u[1]
        full = [("read", *u[1:])] * ((i + 1) % {"exp": LT, "tanh": 4 * LT, "relu": FB}[kind] == 0)
        if kind == "relu":
            out.extend(full)
            full = []

    for s in steps:
        if s[0] in ELEMENT_KINDS:
            out.append(s)
            waiting.append(("use", s, False))
            if len(waiting) > LAG:
                use()
            continue
        needs = {"norm": "exp", "mix": "tanh", "fin": "relu"}.get(s[0])
        while any(w[1][0] == needs for w in waiting):
            use()
        if needs:
            out.extend(full)
            full = []
        out.append(s)
    while last and waiting:
        use()
    return out + full


def build(nc, A):
    with ExitStack() as ctx:
        def sb(name, shape, dt=F32):
            return ctx.enter_context(nc.sbuf_tensor(name, shape, dt))

        def sem(name):
            return ctx.enter_context(nc.semaphore(name))

        con = sb("con", [P, C_W])
        wqk = sb("wqk", [P, 2 * P])
        wv = sb("wv", [P, ATT * C])
        wr = sb("wr", [P, EX])
        brb = sb("brb", [P, EX])
        ag = sb("ag", [P, 2])
        b1T = sb("b1T", [P, EX * FB])
        b2T = sb("b2T", [P, EX])
        b2e = sb("b2e", [EX, D])
        biasT = sb("biasT", [DK, H])
        clsr = sb("clsr", [B, D])
        clsx = sb("clsx", [B, D])
        w1h, w1l = sb("w1h", [P, EX, F], F32R), sb("w1l", [P, EX, F], F32R)
        w2h, w2l = sb("w2h", [P, EX, F], F32R), sb("w2l", [P, EX, F], F32R)
        mh, ml = sb("mh", [P, H, P], F32R), sb("ml", [P, H, P], F32R)
        u = sb("u", [P, H])
        rreph, rrepl = sb("rreph", [P, P], F32R), sb("rrepl", [P, P], F32R)
        greph, grepl = sb("greph", [P, P], F32R), sb("grepl", [P, P], F32R)
        kc = sb("kc", [DK, H])
        cc = sb("cc", [P, 24])
        xin = sb("xin", [P, L])
        trnd = sb("trnd", [P, L], F32R)
        kz = sb("kz", [P, ATT, L], F32R)
        kk = sb("kk", [P, L], F32R)
        qs = sb("qs", [P, L], F32R)
        v1h, v1l = sb("v1h", [P, LT * ATT, VW], F32R), sb("v1l", [P, LT * ATT, VW], F32R)
        nm = sb("nm", [P, LT, P])
        e = sb("e", [P, RING, L])
        eh, el = sb("eh", [P, RING, L], F32R), sb("el", [P, RING, L], F32R)
        ot = sb("ot", [P, ATT, L])
        h1, h2 = sb("h1", [P, LT, D]), sb("h2", [P, LT, D])
        x = sb("x", [P, LT, D])
        xT = sb("xT", [P, L])
        xh, xl = sb("xh", [P, L], F32R), sb("xl", [P, L], F32R)
        yh, yl = sb("yh", [P, L], F32R), sb("yl", [P, L], F32R)
        vz = sb("vz", [P, LT, H, P], F32R)
        gf = sb("gf", [P, L])
        gh, gl = sb("gh", [P, 2, L], F32R), sb("gl", [P, 2, L], F32R)
        tk, tq = sb("tk", [P, L]), sb("tq", [P, L])
        sm = sb("sm", [P, 192])
        mx8 = sb("mx8", [P, LT, 8])
        ix8 = sb("ix8", [P, LT, 8], U32)
        rt = sb("rt", [P, 4, LT, EX])
        cwT = sb("cwT", [EX, L])
        mo = sb("mo", [P, 4, L])
        acc = sb("acc", [P, L])
        outs = sb("outs", [P, LT, D])
        colc = sb("colc", [P, B])
        tl = sb("tl", [P, B])
        cwd = nc.dram_tensor("cwd", [EX, L], F32).ap()

        W = ctx.enter_context(nc.psum_tensor("W", [P, RING, L], F32))
        AC = ctx.enter_context(nc.psum_tensor("AC", [P, 2, L], F32))
        M = ctx.enter_context(nc.psum_tensor("M", [P, L], F32))
        Y = ctx.enter_context(nc.psum_tensor("Y", [P, L], F32))

        ident = con[:, C_ID:C_ID + P]
        AT = ot[:, 2:4, :]
        wqT, wkT = (ot[0:DK, 2 * k:2 * k + 2, :].rearrange("p a (h d) -> p (a h) d", d=P) for k in range(2))
        cwb, prod = mo[:, 0:2, :], mo[:, 2:4, :]
        hc = x[0:B, 2, :]
        hid32, hidh, hidl = gf[:, 0:EX * FB * B], gh[:, 0, 0:EX * FB * B], gl[:, 0, 0:EX * FB * B]
        diag = tq[0:B, 0:EX * B]
        xcT = tl[:]
        padded = vz[:].rearrange("p t h c -> p (t h c)")
        xce = padded[:, 0:EX * (P + 2 * B)].rearrange("p (e c) -> p e c", c=P + 2 * B)
        FIRST = ((con, "consts"), (wqk, "wqk"), (wv, "wv"))
        SMALL = ((wqT, "wqT"), (wkT, "wkT"), (wr, "wr"), (brb, "brb"),
                 (ag, "ag"), (b1T, "b1T"), (b2T, "b2T"), (b2e, "b2"), (biasT, "biasT"),
                 (clsr, "cls"), (xT, "wk"))

        first_in = sem("first_in")
        consts_in = sem("consts_in")
        wts_in = [sem(f"wts_in{i}") for i in range(4)]
        wts_hi = sem("wts_hi")
        wts_lo = sem("wts_lo")
        pool_set = sem("pool_set")
        setup_pe, setup_dve, setup_act = sem("setup_pe"), sem("setup_dve"), sem("setup_act")
        shift_rows = sem("shift_rows")
        k_ready = sem("k_ready")
        kz_ready = sem("kz_ready")
        h2_ready = sem("h2_ready")
        xin_ready = sem("xin_ready")
        w_ready = sem("w_ready")
        w_read = [sem(f"w_read{i}") for i in range(RING)]
        m_ready = sem("m_ready")
        m_read = sem("m_read")
        ac_read = [sem("ac_read0"), sem("ac_read1")]
        parts_ready = sem("parts_ready")
        v1_hi = sem("v1_hi")
        parts_used = sem("parts_used")
        rounded = sem("rounded")
        shift_ready = sem("shift_ready")
        var_ready = sem("var_ready")
        rstd_ready = sem("rstd_ready")
        x_ready = sem("x_ready")
        vz_hi, vz_ready = sem("vz_hi"), sem("vz_ready")
        xp_ready = sem("xp_ready")
        yp_ready = sem("yp_ready")
        g_ready = sem("g_ready")
        ck_ready = sem("ck_ready")
        logits_ready = sem("logits_ready")
        ex_ready = sem("ex_ready")
        cw_ready = sem("cw_ready")
        cwd_done = sem("cwd_done")
        cwb_ready = [sem("cwb_ready0"), sem("cwb_ready1")]
        prod_ready = sem("prod_ready")
        acc_added = sem("acc_added")
        fin_ready = sem("fin_ready")
        out_ready = sem("out_ready")
        out_done = sem("out_done")
        carried = sem("carried")
        chain = sem("chain")
        cls_pe, cls_dve = sem("cls_pe"), sem("cls_dve")
        cls_act, cls_pool = sem("cls_act"), sem("cls_pool")
        cls_stored = sem("cls_stored")

        credit = [(prod_ready, 2), (acc_added, 2), (out_ready, 1), (fin_ready, 1), (out_done, 16)]

        def wait(eng, s, n, per, k):
            base, off = n if isinstance(n, tuple) else (0, n)
            k += off * per + sum(c for t, c in credit if t is s)
            if not isinstance(base, int) or base * per + k > 0:
                eng.wait_ge(s, base * per + k)

        def fixed(n):
            return isinstance(n, int)

        W_KINDS = {"k": 1, "q": 1, "v": 1, "max": 1, "shift": 1, "norm": 1, "exp": 1, "tanh": 1, "relu": 1}

        def positions(steps):
            w_at, e_at, w, e_ = {}, {}, 0, 0
            for s in steps:
                w_at[s], e_at[s] = w, e_
                w += W_KINDS.get(s[0], 0)
                e_ += s[0] in ELEMENT_KINDS
            return w_at, e_at, w, e_

        def slots_before(w):
            return [(w + RING - 1 - j) // RING for j in range(RING)]

        _, _, NW, NE = positions(ORDER)
        NWS = slots_before(NW)

        class Round:

            def __init__(self, steps, b, full, w0, ws0, e0, before=None, last=False):
                plus = (lambda k: b + k) if isinstance(b, int) else (lambda k: (b[0], b[1] + k))
                self.n, self.n1, self.m = plus(0), plus(1), plus(-1)
                self.before = before
                self.steps = with_uses(before.plain if before else [], steps, last)
                self.plain = steps
                self.w_at, self.e_at, w, e_ = positions(steps)
                self.full, self.w0, self.ws0, self.e0 = full, w0, ws0, e0
                self.after = (w0 + w, [a + c for a, c in zip(ws0, slots_before(w))], e0 + e_)
                assert e0 % RING == NE % RING == 0

            def batch(self, relu):
                return self.n if relu < LATE else self.m

            def used(self, step):
                return (self.before if step[2] else self), step[1]

            def slot(self, step, j=0):
                return (self.w_at[step] + j) % RING

            def eslot(self, step):
                return self.e_at[step] % RING

            def wait_full(self, eng, step, j=0):
                wait(eng, w_ready, self.full, NW, self.w0 + self.w_at[step] + j + 1)

            def wait_read(self, eng, step, j=0, before=0):
                k = self.slot(step, j)
                wait(eng, w_read[k], self.full, NWS[k], self.ws0[k] + (self.w_at[step] + j) // RING + 1 - before)

            def wait_e(self, eng, s, step, before=0):
                wait(eng, s, self.full, NE, self.e0 + self.e_at[step] + 1 - before)

        r0 = Round(FIRST_HALF, -1, 0, 0, [0] * RING, 0)
        r1 = Round(NO_EARLY, 0, 0, *r0.after, r0)
        START = r1.after
        LOOP = B - 2
        r7 = Round(ORDER, B - 2, LOOP - 1, *START)
        r8 = Round(NO_FIRST, B - 1, LOOP, *START, r7)
        r9 = Round(LAST, B, LOOP, *r8.after, r8, last=True)

        def rounds(eng, body):
            body(r0)
            body(r1)
            with eng.Fori(1, B - 1) as b:
                body(Round(ORDER, (b, 0), (b, -1), *START, Round(ORDER, (b, -1), (b, -2), *START)))
            body(r8)
            body(r9)

        def output_of(batch, ex):
            return AC[:, 1, :] if batch == B - 1 and ex % 2 else Y[:]

        def apart(eng):
            eng.sem_inc(carried, 1)

        MU = {"xT": 1, "tk": 2, "tq": 3, "g": 4, "mix": 12, "yT": 13, "logits": 14, "cwT": 15}
        NM = 15
        XC, BK, TCC, CCX, T1, LOGIT = 0, 1, 2, 3, 4, 5
        VAR, RSTD, MV, BN = 8, 9, 10, 12
        S_BN, S_MV, S_VE, S_RS, S_DEN, S_MX, S_SX, S_ST, S_SB, S_R = 0, 24, 32, 36, 48, 64, 80, 81, 82, 96
        nhalf = con[:, C_NHALF:C_NHALF + 1]
        urep, rrep, grep = tq[:, 0:P], tk[:, 0:P], tk[:, P:2 * P]

        block = ctx.enter_context(nc.Block())

        @block.sync
        def _(sp):
            sp.sem_inc(out_done, 16)
            for dst, src in FIRST:
                sp.dma_start(dst[:], A[src]).then_inc(first_in, 16)
            sp.dma_start(xin[:], A["xT"][0]).then_inc(xin_ready, 16)
            for dst, src in SMALL:
                sp.dma_start(dst[:], A[src]).then_inc(consts_in, 16)

            def spread(ex, n):
                wait(sp, prod_ready, n, EX, ex - 1)
                sp.dma_start(cwb[:, ex % 2, :], cwd[ex:ex + 1, :].partition_broadcast(P)
                             ).then_inc(cwb_ready[ex % 2], 16)

            def load_weights(c):
                if c >= 4:
                    sp.wait_ge(wts_lo, c - 3)
                if c < 2 * EX:
                    src = A["w1"][:, c, :] if c < EX else A["w2"][:, c - EX, :]
                    sp.dma_start(mo[:, c % 4, :], src).then_inc(wts_in[c % 4], 16)

            for c in range(4):
                load_weights(c)

            def body(r):
                n, n1, m = r.n, r.n1, r.m
                for s in r.steps:
                    if r is r1 and s[0] == "tanh" and s[1] % 2 == 0:
                        load_weights(s[1] // 2 + 4)
                    if s == ("v", 1):
                        r.wait_full(sp, s)
                        if fixed(n1):
                            sp.dma_start(xin[:], A["xT"][n1 + 1]).then_inc(xin_ready, 16)
                        else:
                            sp.dma_start(xin[:], A["xT"][bass.ds(n1[0] + (n1[1] + 1), 1)].rearrange("a p n -> p (a n)")
                                         ).then_inc(xin_ready, 16)
                    if s[0] == "relu" and s[1] % FB == FB - 1 and s[1] // FB + 2 < EX:
                        spread(s[1] // FB + 2, r.batch(s[1]))
                    if s == ("cls", 7):
                        sp.wait_ge(cls_dve, 8)
                        sp.dma_start(A["out"][:, 0, :], x[0:B, 3, :]).then_inc(cls_stored, 16)
                    if s[0] == "out":
                        if fixed(m):
                            dst = A["out"][m, 1:L + 1, :].rearrange("(t p) d -> p t d", p=P)
                        else:
                            dst = A["out"][bass.ds(m[0] + m[1], 1), 1:L + 1, :].rearrange("a (t p) d -> p (a t) d", p=P)
                        wait(sp, out_ready, m, 1, 1)
                        sp.dma_start(dst, outs[:]).then_inc(out_done, 16)
                    if s[0] == "cwT":
                        wait(sp, m_read, n, NM, MU["cwT"])
                        for k in range(2):
                            apart(sp)
                            wait(sp, cwb_ready[k], m, 8 * EX, 8 * EX)
                        sp.dma_start(cwd, cwT[:]).then_inc(cwd_done, 16)
                        wait(sp, cwd_done, n, 16, 16)
                        for ex in range(2):
                            apart(sp)
                            spread(ex, n)

            rounds(sp, body)
            sp.wait_ge(cls_stored, 16)
            sp.wait_ge(out_done, 16 * (B + 1))
            sp.wait_ge(cwd_done, 16 * B)
            sp.wait_ge(xin_ready, 16 * (B + 1))

        @block.gpsimd
        def _(pool):
            g = nc.gpsimd
            pool.sem_inc(acc_added, 2)
            g.memset(nm[:], 0.0)
            g.memset(v1h[:].bitcast(F32), 1.0)
            g.memset(v1l[:].bitcast(F32), 0.0).then_inc(pool_set, 1)
            g.memset(vz[:].bitcast(F32), 0.0).then_inc(pool_set, 1)
            pool.wait_ge(first_in, 16 * len(FIRST))

            def split_weights(c):
                pool.wait_ge(wts_hi, c + 1)
                hi, lo = (w1h, w1l) if c < EX else (w2h, w2l)
                g.tensor_tensor(lo[:, c % EX, :], mo[:, c % 4, :], hi[:, c % EX, :], ALU.subtract).then_inc(wts_lo, 1)

            def rstd(n, k):
                wait(pool, var_ready, n, 2, k + 1)
                g.tensor_tensor(sm[:, S_RS:S_RS + LT], sm[:, S_VE:S_VE + LT], nhalf.to_broadcast([P, LT]),
                                ALU.pow).then_inc(rstd_ready, 1)

            def values(n):
                wait(pool, x_ready, n, 2, 1)
                if n == 0:
                    pool.wait_ge(pool_set, 2)
                if not fixed(n):
                    wait(pool, m_read, n, NM, 0)
                    apart(pool)
                for lo in range(2):
                    for t in range(LT):
                        xv = x[:, t, :].rearrange("p (k q d) -> p k q d", k=2, q=4)
                        v = vz[:, t, :, :].rearrange("p (k q) c -> p k (q c)", k=2)
                        for q in range(4):
                            at = q * P + q * 2 * DV
                            if lo:
                                ins = g.tensor_tensor(v[:, :, at + DV:at + 2 * DV], xv[:, :, q, :],
                                                      v[:, :, at:at + DV], ALU.subtract)
                            else:
                                ins = g.tensor_copy(v[:, :, at:at + DV], xv[:, :, q, :])
                    if lo:
                        ins.then_inc(vz_ready, 1)
                    else:
                        ins.then_inc(vz_hi, 1)
                        wait(pool, vz_hi, n, 1, 1)

            def body(r):
                for s in r.steps:
                    if s == ("setup", 0):
                        pool.wait_ge(var_ready, 1)
                        g.tensor_tensor(cc[0:B, RSTD:RSTD + 1], cc[0:B, VAR:VAR + 1], nhalf[0:B], ALU.pow
                                        ).then_inc(rstd_ready, 1)
                    if s == ("cls", 0):
                        wait(pool, m_ready, B - 1, NM, MU["mix"])
                        g.memset(padded[:, 0:EX * P].bitcast(F32), 0.0).then_inc(pool_set, 1)
                    if s == ("cls", 1):
                        wait(pool, var_ready, B, 2, 2)
                        g.tensor_tensor(cc[0:B, RSTD:RSTD + 1], cc[0:B, VAR:VAR + 1], nhalf[0:B], ALU.pow
                                        ).then_inc(cls_pool, 1)
                    if r is r1 and s[0] == "tanh" and s[1] % 2 == 0:
                        split_weights(s[1] // 2)
                    if s == ("norm", LT - 1):
                        rstd(r.n, 1)
                    if s[0] == "ln1":
                        values(r.n)
                    if s[0] == "mid":
                        rstd(r.n, 2)
                    if s[0] == "ln2":
                        wait(pool, out_ready, r.m, 1, 1)
                        apart(pool)
                        wait(pool, m_read, r.n, NM, MU["mix"])
                        apart(pool)
                        g.tensor_copy(h2[:], h1[:]).then_inc(h2_ready, 1)
                    if s[0] == "k":
                        wait(pool, k_ready, r.n1, 1, 1)
                        apart(pool)
                        for a in range(ATT):
                            own = con[:, C_OWN + a:C_OWN + a + 1].to_broadcast([P, L])
                            ins = g.tensor_tensor(kz[:, a, :], kk[:], own, ALU.mult)
                        ins.then_inc(kz_ready, 1)
                    if s[0] == "read" and s[1][0] == "relu":
                        o, s = r.used(s)
                        ex, b = s[1] // FB, o.batch(s[1])
                        wait(pool, prod_ready, b, EX, ex + 1)
                        if ex == 0:
                            wait(pool, fin_ready, b, 1, 0)
                            apart(pool)
                            g.tensor_copy(acc[:], prod[:, 0, :]).then_inc(acc_added, 1)
                        else:
                            wait(pool, acc_added, b, EX, ex)
                            g.tensor_tensor(acc[:], acc[:], prod[:, ex % 2, :], ALU.add).then_inc(acc_added, 1)

            rounds(pool, body)

        @block.scalar
        def _(act):
            a = nc.scalar
            act.wait_ge(first_in, 16 * len(FIRST))

            def split_weights(c):
                act.wait_ge(wts_in[c % 4], 16 * (c // 4 + 1))
                a.copy((w1h if c < EX else w2h)[:, c % EX, :], mo[:, c % 4, :]).then_inc(wts_hi, 1)

            def elements(r, s):
                kind, i = s
                slot, es = r.slot(s), r.eslot(s)
                fn, args = {"exp": (ACT.Exp, {"scale": float(DQ) ** -0.5}), "tanh": (ACT.Tanh, {"scale": 0.5}),
                            "relu": (ACT.Relu, {"bias": b1T[:, i:i + 1]})}[kind]
                r.wait_full(act, s)
                r.wait_e(act, parts_ready, s, RING)
                a.activation(e[:, es, :], W[:, slot, :], fn, **args)
                r.wait_e(act, parts_used, s, RING)
                a.activation(eh[:, es, :], W[:, slot, :], fn, **args).then_inc(w_read[slot], 1)

            def body(r):
                n, n1 = r.n, r.n1
                for s in r.steps:
                    if r is r1 and s[0] == "tanh" and s[1] % 2 == 0:
                        split_weights(s[1] // 2)
                    if s == ("setup", 5):
                        act.wait_ge(setup_dve, 6)
                        a.activation(cc[:, TCC:TCC + 1], cc[:, LOGIT:LOGIT + 1], ACT.Tanh, scale=0.5
                                     ).then_inc(setup_act, 1)
                    elif s == ("cls", 4):
                        act.wait_ge(cls_dve, 4)
                        a.activation(rt[0:B, 1, 0, :], rt[0:B, 0, 0, :], ACT.Exp).then_inc(cls_act, 1)
                    elif s[0] in ELEMENT_KINDS:
                        elements(r, s)
                    elif s[0] == "read" and s[1][0] == "exp":
                        o, u_ = r.used(s)
                        at = u_[1] // LT
                        o.wait_e(act, parts_used, u_)
                        if at == 2:
                            wait(act, m_ready, o.n, NM, MU["mix"])
                        a.copy(ot[0:C + 1, at, :], AC[0:C + 1, at % 2, :]).then_inc(ac_read[at % 2], 1)
                    elif s[0] == "read" and s[1][0] == "tanh":
                        o, u_ = r.used(s)
                        k = u_[1] // (4 * LT)
                        o.wait_e(act, parts_used, u_)
                        a.copy(AT[:, k, :], AC[:, k, :]).then_inc(ac_read[k], 1)
                    elif s[0] == "k":
                        r.wait_full(act, s)
                        a.activation(trnd[:], W[:, r.slot(s), :], ACT.Identity,
                                     bias=con[:, C_ONE:C_ONE + 1]).then_inc(rounded, 1)
                    elif s[0] == "q":
                        r.wait_full(act, s)
                        r.wait_read(act, ("k", 0))
                        a.copy(trnd[:], W[:, r.slot(s), :]).then_inc(rounded, 1)
                    elif s[0] == "shift":
                        r.wait_full(act, s)
                        a.copy(trnd[:], W[:, r.slot(s), :]).then_inc(rounded, 1)
                    elif s[0] == "xT":
                        wait(act, m_ready, n, NM, MU["xT"])
                        a.activation(xT[:], M[:], ACT.Identity, accum_out=sm[:, S_SX:S_SX + 1]).then_inc(m_read, 1)
                    elif s[0] == "tk":
                        wait(act, m_ready, n, NM, MU["tk"])
                        a.activation(tk[:], M[:], ACT.Tanh, scale=0.5, bias=cc[:, BK:BK + 1]).then_inc(m_read, 1)
                    elif s[0] == "tq":
                        wait(act, m_ready, n, NM, MU["tq"])
                        a.activation(tq[:], M[:], ACT.Tanh, scale=0.5).then_inc(m_read, 1)
                    elif s[0] == "g":
                        h = s[1]
                        wait(act, m_ready, n, NM, MU["g"] + h)
                        wait(act, g_ready, n, H, h)
                        a.activation(gf[:], M[:], ACT.Identity, bias=u[:, h:h + 1]).then_inc(m_read, 1)
                    elif s[0] == "yT":
                        wait(act, m_ready, n, NM, MU["yT"])
                        a.copy(xT[:], M[:]).then_inc(m_read, 1)
                    elif s[0] == "logits":
                        wait(act, logits_ready, n, 1, 1)
                        a.activation(rt[:, 1, :, :], rt[:, 0, :, :], ACT.Exp).then_inc(ex_ready, 1)
                    elif s[0] == "cwT":
                        wait(act, m_ready, n, NM, MU["cwT"])
                        wait(act, cwd_done, n, 16, 0)
                        a.copy(cwT[:], M[0:EX, :]).then_inc(m_read, 1)

            rounds(act, body)

        @block.vector
        def _(dve):
            v = nc.vector
            dve.sem_inc(prod_ready, 2)
            dve.sem_inc(out_ready, 1)
            links, setup_links = [0], [0]

            def link(ins, n=0, per=0):
                links[0] += 1
                ins.then_inc(chain, 1)
                wait(dve, chain, n, per, links[0])

            def moments(src, tiles, rows, bn, mv, ve, n, per):
                for t in range(tiles):
                    ins = v.bn_stats(bn[0:rows, 6 * t:6 * t + 6], src(t))
                link(ins, n, per)
                apart(dve)
                for t in range(tiles):
                    ins = v.bn_aggr(mv[0:rows, 2 * t:2 * t + 2], bn[0:rows, 6 * t:6 * t + 6])
                link(ins, n, per)
                v.tensor_scalar(ve[0:rows, 0:tiles], mv[0:rows, 1:2 * tiles:2], LN_EPS, None, ALU.add
                                ).then_inc(var_ready, 1)

            def normalise(src, dst, tiles, rows, mv, rs):
                for t in range(tiles):
                    ins = v.tensor_scalar(dst(t), src(t), mv[0:rows, 2 * t:2 * t + 1], rs[0:rows, t:t + 1],
                                          ALU.subtract, ALU.mult)
                return ins

            def less_maximum(rows, T, n, per, signal):
                r0_, mxs = rt[0:rows, 0, 0:T, :], sm[0:rows, S_MX:S_MX + T]
                link(v.tensor_reduce(mxs, r0_, AX_X, ALU.max), n, per)
                v.tensor_tensor(r0_, r0_, mxs.unsqueeze(2).to_broadcast([rows, T, EX]), ALU.subtract
                                ).then_inc(signal, 1)

            def top2(rows, T, n, per):
                r0_, r1_, r2_, r3_ = (rt[0:rows, i, 0:T, :] for i in range(4))
                den = sm[0:rows, S_R:S_R + T]
                link(v.tensor_reduce(den, r1_, AX_X, ALU.add), n, per)
                link(v.reciprocal(den, den), n, per)
                link(v.tensor_tensor(r1_, r1_, den.unsqueeze(2).to_broadcast([rows, T, EX]), ALU.mult), n, per)
                apart(dve)
                for t in range(T):
                    ins = v.max(mx8[0:rows, t, :], rt[0:rows, 1, t, :])
                link(ins, n, per)
                apart(dve)
                for t in range(T):
                    ins = v.max_index(ix8[0:rows, t, :], mx8[0:rows, t, :], rt[0:rows, 1, t, :])
                link(ins, n, per)
                iota = con[0:rows, C_IOTA:C_IOTA + EX].unsqueeze(1).to_broadcast([rows, T, EX])
                v.tensor_tensor(r2_, iota, ix8[0:rows, 0:T, 0:1].to_broadcast([rows, T, EX]), ALU.is_equal)
                link(v.tensor_tensor(r3_, iota, ix8[0:rows, 0:T, 1:2].to_broadcast([rows, T, EX]), ALU.is_equal),
                     n, per)
                link(v.tensor_tensor(r2_, r2_, r3_, ALU.add), n, per)
                return v.tensor_tensor(r0_, r2_, r1_, ALU.mult)

            dve.wait_ge(first_in, 16 * len(FIRST))
            dve.wait_ge(pool_set, 1)

            def setup(k):
                if k == 0:
                    dve.wait_ge(consts_in, 16 * len(SMALL))
                    moments(lambda t: clsr[:], 1, B, cc[:, BN:BN + 6], cc[:, MV:MV + 2], cc[:, VAR:VAR + 1], 0, 0)
                    dve.wait_ge(setup_pe, 2)
                    for k, m32 in enumerate((h1, h2)):
                        v.tensor_scalar(m32[:], AC[:, k, :].rearrange("p (h d) -> p h d", h=4), float(DK) ** -0.5, None,
                                        ALU.mult)
                    link(v.tensor_copy(u[:], Y[:, 0:H]))
                    v.tensor_copy(urep.rearrange("p (h d) -> p h d", h=H), u[:].unsqueeze(2).to_broadcast([P, H, DV]))
                    dve.wait_ge(rstd_ready, 1)
                    normalise(lambda t: clsr[:], lambda t: clsx[:], 1, B, cc[:, MV:MV + 2], cc[:, RSTD:RSTD + 1]
                              ).then_inc(setup_dve, 1)
                elif k == 1:
                    v.tensor_copy(mh[:, 0:4, :], h1[:])
                    link(v.tensor_copy(mh[:, 4:8, :], h2[:]))
                    v.tensor_tensor(ml[:, 0:4, :], h1[:], mh[:, 0:4, :], ALU.subtract)
                    v.tensor_tensor(ml[:, 4:8, :], h2[:], mh[:, 4:8, :], ALU.subtract).then_inc(setup_dve, 1)
                    dve.wait_ge(setup_pe, 3)
                    v.tensor_copy(cc[:, XC:XC + 1], M[:, 0:1]).then_inc(setup_dve, 1)
                elif k == 2:
                    dve.wait_ge(setup_pe, 4)
                    v.tensor_copy(kc[:], M[0:DK, 0:H]).then_inc(setup_dve, 1)
                elif k == 3:
                    dve.wait_ge(setup_pe, 5)
                    v.tensor_scalar(rrep.rearrange("p (h d) -> p h d", h=H),
                                    M[:, 0:H].unsqueeze(2).to_broadcast([P, H, DV]), float(DK) ** -0.5, None, ALU.mult)
                    v.tensor_tensor(grep.rearrange("p (h d) -> p h d", h=H),
                                    M[:, H:2 * H].unsqueeze(2).to_broadcast([P, H, DV]),
                                    u[:].unsqueeze(2).to_broadcast([P, H, DV]), ALU.add).then_inc(setup_dve, 1)
                elif k == 4:
                    dve.wait_ge(setup_pe, 6)
                    v.tensor_copy(rreph[:], rrep)
                    link(v.tensor_copy(greph[:], grep))
                    v.tensor_tensor(rrepl[:], rrep, rreph[:], ALU.subtract)
                    v.tensor_tensor(grepl[:], grep, greph[:], ALU.subtract)
                    v.tensor_scalar(cc[:, BK:BK + 1], M[:, 0:1], 0.5, None, ALU.mult)
                    v.tensor_copy(cc[:, LOGIT:LOGIT + 1], M[:, 1:2]).then_inc(setup_dve, 1)
                else:
                    dve.wait_ge(setup_act, 1)
                    link(v.tensor_scalar(cc[:, T1:T1 + 1], cc[:, TCC:TCC + 1], 1.0, None, ALU.add))
                    link(v.tensor_tensor(cc[:, CCX:CCX + 1], cc[:, T1:T1 + 1], cc[:, XC:XC + 1], ALU.mult))

            def class_tokens(k):
                if k == 0:
                    v.tensor_scalar(colc[:], colc[:], cc[:, CCX:CCX + 1], 0.5, ALU.add, ALU.mult).then_inc(cls_dve, 1)
                elif k == 1:
                    dve.wait_ge(cls_pe, 1)
                    link(v.tensor_tensor(hc, clsr[:], M[0:B, 0:P], ALU.add))
                    moments(lambda t: hc, 1, B, cc[:, BN:BN + 6], cc[:, MV:MV + 2], cc[:, VAR:VAR + 1], 0, 0)
                elif k == 2:
                    dve.wait_ge(cls_pool, 1)
                    normalise(lambda t: hc, lambda t: clsx[:], 1, B, cc[:, MV:MV + 2], cc[:, RSTD:RSTD + 1]
                              ).then_inc(cls_dve, 1)
                elif k == 3:
                    dve.wait_ge(cls_pe, 2)
                    dve.wait_ge(pool_set, 3)
                    link(v.tensor_copy(xcT, M[:, 0:B]))
                    every = xcT.unsqueeze(1).to_broadcast([P, EX, B])
                    link(v.tensor_copy(xce[:, :, 0:B], every))
                    v.tensor_tensor(xce[:, :, B:2 * B], every, xce[:, :, 0:B], ALU.subtract).then_inc(cls_dve, 1)
                elif k == 4:
                    dve.wait_ge(cls_pe, 3)
                    link(v.tensor_tensor(rt[0:B, 0, 0, :], M[0:B, 0:EX], brb[0:B, :], ALU.add))
                    less_maximum(B, 1, 0, 0, cls_dve)
                    dve.wait_ge(cls_pe, 4)
                    v.tensor_copy(gf[:], AC[:, 0, :]).then_inc(cls_dve, 1)
                elif k == 5:
                    dve.wait_ge(cls_act, 1)
                    link(top2(B, 1, 0, 0))
                    v.tensor_tensor(diag.rearrange("p (e b) -> p e b", b=B),
                                    rt[0:B, 0, 0, :].unsqueeze(2).to_broadcast([B, EX, B]),
                                    ident[0:B, 0:B].unsqueeze(1).to_broadcast([B, EX, B]), ALU.mult
                                    ).then_inc(cls_dve, 1)
                elif k == 6:
                    dve.wait_ge(cls_pe, 5)
                    b1 = b1T[:].rearrange("p (e f) -> p f e", f=FB)
                    for f in range(FB):
                        c = slice(f * EX * B, (f + 1) * EX * B)
                        ins = v.tensor_tensor(hid32[:, c].rearrange("p (e b) -> p e b", b=B),
                                              M[:, c].rearrange("p (e b) -> p e b", b=B),
                                              b1[:, f, :].unsqueeze(2).to_broadcast([P, EX, B]), ALU.add)
                    link(ins)
                    link(v.tensor_scalar(hid32, hid32, 0.0, None, ALU.max))
                    dve.wait_ge(cls_pe, 6)
                    v.tensor_copy(cwT[:, 0:B], AC[0:EX, 0, EX * B:EX * B + B])
                    h3 = hid32.rearrange("p (f c) -> p f c", f=FB)
                    link(v.tensor_tensor(h3, h3, AC[:, 0, 0:EX * B].unsqueeze(1).to_broadcast([P, FB, EX * B]),
                                         ALU.mult))
                    link(v.tensor_copy(hidh, hid32))
                    v.tensor_tensor(hidl, hid32, hidh, ALU.subtract).then_inc(cls_dve, 1)
                else:
                    dve.wait_ge(cls_pe, 7)
                    v.tensor_tensor(x[0:B, 3, :], hc, M[0:B, 0:D], ALU.add).then_inc(cls_dve, 1)

            def split(r, s):
                es = r.eslot(s)
                r.wait_read(dve, s)
                r.wait_e(dve, parts_used, s, RING)
                v.tensor_tensor(el[:, es, :], e[:, es, :], eh[:, es, :], ALU.subtract).then_inc(parts_ready, 1)

            def body(r):
                n, n1, m = r.n, r.n1, r.m
                links[0] = setup_links[0] + (B * CHAIN if r is r9 else 0)
                for s in r.steps:
                    per = CHAIN
                    if s[0] == "setup":
                        setup(s[1])
                    elif s[0] == "cls":
                        class_tokens(s[1])
                    elif s[0] in ELEMENT_KINDS:
                        split(r, s)
                    elif s[0] == "read" and s[1][0] == "relu":
                        o, u_ = r.used(s)
                        ex, b = u_[1] // FB, o.batch(u_[1])
                        o.wait_e(dve, parts_used, u_)
                        wait(dve, cwb_ready[ex % 2], b, 8 * EX, 16 * (ex // 2 + 1))
                        wait(dve, acc_added, b, EX, ex - 1)
                        v.scalar_tensor_tensor(prod[:, ex % 2, :], output_of(b, ex), b2T[:, ex:ex + 1],
                                               cwb[:, ex % 2, :], ALU.add, ALU.mult).then_inc(prod_ready, 1)
                    elif s[0] == "out":
                        wait(dve, fin_ready, m, 1, 1)
                        wait(dve, out_done, m, 16, 0)
                        wait(dve, h2_ready, m, 1, 1)
                        v.tensor_tensor(outs[:].rearrange("p t d -> p (t d)"), Y[:],
                                        h2[:].rearrange("p t d -> p (t d)"), ALU.add).then_inc(out_ready, 1)
                    elif s[0] == "k":
                        wait(dve, rounded, n1, 3, 1)
                        wait(dve, kz_ready, n1, 1, 0)
                        v.scalar_tensor_tensor(kk[:], trnd[:], con[:, C_MK:C_MK + 1], W[:, r.slot(s), :], ALU.mult,
                                               ALU.add).then_inc(w_read[r.slot(s)], 1)
                        r.wait_read(dve, s)
                        dve.sem_inc(k_ready, 1)
                    elif s[0] == "q":
                        wait(dve, rounded, n1, 3, 2)
                        v.scalar_tensor_tensor(qs[:], trnd[:], con[:, C_MQ:C_MQ + 1], W[:, r.slot(s), :], ALU.mult,
                                               ALU.add).then_inc(w_read[r.slot(s)], 1)
                    elif s[0] == "v":
                        r.wait_full(dve, s)
                        vv = W[:, r.slot(s), :].rearrange("p (g c) -> p g c", c=C)
                        g8 = slice(2 * ATT * s[1], 2 * ATT * (s[1] + 1))
                        v.tensor_copy(v1h[:, g8, 0:C], vv).then_inc(v1_hi, 1)
                        wait(dve, v1_hi, n1, 2, s[1] + 1)
                        v.tensor_tensor(v1l[:, g8, 0:C], vv, v1h[:, g8, 0:C], ALU.subtract
                                        ).then_inc(w_read[r.slot(s)], 1)
                    elif s[0] == "max":
                        t, at = divmod(s[1], ATT)
                        c0 = at * ROWS + SHIFT
                        slot = r.slot(s)
                        r.wait_full(dve, s)
                        v.tensor_reduce(nm[:, t, c0:c0 + 1], W[:, slot, :], AX_X, ALU.max, negate=True
                                        ).then_inc(w_read[slot], 1)
                    elif s[0] == "neg":
                        for k in range(RING):
                            r.wait_read(dve, ("max", LT * ATT - 1 - k))
                        v.tensor_copy(nm[:, :, SHIFT + 1::ROWS], nm[:, :, SHIFT::ROWS]).then_inc(shift_ready, 1)
                    elif s[0] == "qshift":
                        slot = r.slot(("shift", 0))
                        wait(dve, rounded, n1, 3, 3)
                        v.scalar_tensor_tensor(kk[:], trnd[:], con[:, C_MQ:C_MQ + 1], W[:, slot, :], ALU.mult, ALU.add
                                               ).then_inc(shift_rows, 1)
                        wait(dve, shift_rows, n1, 1, 1)
                        v.tensor_tensor(qs[:], qs[:], kk[:], ALU.add).then_inc(w_read[slot], 1)
                    elif s[0] == "norm":
                        t, slot = s[1], r.slot(s)
                        r.wait_full(dve, s)
                        wait(dve, h2_ready, n, 1, 0)
                        o = W[:, slot, 0:ATT * (C + 1)].rearrange("p (s k c) -> p s k c", s=2, k=2)
                        den = sm[:, S_DEN:S_DEN + 4].rearrange("p (s k) -> p s k", k=2)
                        link(v.reciprocal(den, o[:, :, :, C]), n, per)
                        link(v.tensor_tensor(den[:, :, 0], den[:, :, 0], ag[:], ALU.mult), n, per)
                        hv = h1[:, t, :].rearrange("p (s c) -> p s c", s=2)
                        xv = x[:, t, :].rearrange("p (s c) -> p s c", s=2)
                        v.tensor_tensor(xv, o[:, :, 0, 0:C], den[:, :, 0:1].to_broadcast([P, 2, C]), ALU.mult)
                        v.tensor_tensor(hv, o[:, :, 1, 0:C], den[:, :, 1:2].to_broadcast([P, 2, C]), ALU.mult
                                        ).then_inc(w_read[slot], 1)
                        r.wait_read(dve, s)
                        link(v.tensor_tensor(h1[:, t, :], h1[:, t, :], x[:, t, :], ALU.add), n, per)
                        if t == LT - 1:
                            moments(lambda t: h1[:, t, :], LT, P, sm[:, S_BN:], sm[:, S_MV:], sm[:, S_VE:], n, per)
                    elif s[0] == "ln1":
                        wait(dve, rstd_ready, n, 2, 2)
                        normalise(lambda t: h1[:, t, :], lambda t: x[:, t, :], LT, P, sm[:, S_MV:], sm[:, S_RS:]
                                  ).then_inc(x_ready, 1)
                    elif s[0] == "xp":
                        wait(dve, m_read, n, NM, MU["xT"])
                        link(v.tensor_copy(xh[:], xT[:]), n, per)
                        v.tensor_tensor(xl[:], xT[:], xh[:], ALU.subtract).then_inc(xp_ready, 1)
                        link(v.tensor_tensor(sm[:, S_SB:S_SB + 1], sm[:, S_SX:S_SX + 1], cc[:, XC:XC + 1], ALU.add),
                             n, per)
                    elif s[0] == "tk":
                        wait(dve, m_read, n, NM, MU["tk"])
                        v.tensor_scalar(tk[:], tk[:], cc[:, XC:XC + 1], sm[:, S_SB:S_SB + 1], ALU.mult, ALU.add
                                        ).then_inc(ck_ready, 1)
                    elif s[0] == "tq":
                        wait(dve, m_read, n, NM, MU["tq"])
                        v.tensor_tensor_reduce(out=tq[:], in0=tq[:], in1=xT[:], scale=1.0, scalar=0.0, op0=ALU.mult,
                                               op1=ALU.add, accum_out=sm[:, S_ST:S_ST + 1]).then_inc(chain, 1)
                        links[0] += 1
                        wait(dve, chain, n, per, links[0])
                        dst = colc[:, n:n + 1] if fixed(n) else colc[:, bass.ds(n[0] + n[1], 1)]
                        v.tensor_scalar(dst, sm[:, S_ST:S_ST + 1], sm[:, S_SX:S_SX + 1], None, ALU.add)
                    elif s[0] == "g":
                        h = s[1]
                        wait(dve, m_read, n, NM, MU["g"] + h)
                        if h >= 2:
                            r.wait_full(dve, ("tanh", (h - 1) * LT - 1))
                        link(v.tensor_copy(gh[:, h % 2, :], gf[:]), n, per)
                        v.tensor_tensor(gl[:, h % 2, :], gf[:], gh[:, h % 2, :], ALU.subtract).then_inc(g_ready, 1)
                    elif s[0] == "mid":
                        wait(dve, m_ready, n, NM, MU["mix"])
                        v.tensor_tensor(h1[:].rearrange("p t d -> p (t d)"), M[:],
                                        h1[:].rearrange("p t d -> p (t d)"), ALU.add).then_inc(m_read, 1)
                        wait(dve, m_read, n, NM, MU["mix"])
                        moments(lambda t: h1[:, t, :], LT, P, sm[:, S_BN:], sm[:, S_MV:], sm[:, S_VE:], n, per)
                    elif s[0] == "ln2":
                        wait(dve, rstd_ready, n, 2, 3)
                        wait(dve, vz_ready, n, 1, 1)
                        normalise(lambda t: h1[:, t, :], lambda t: x[:, t, :], LT, P, sm[:, S_MV:], sm[:, S_RS:]
                                  ).then_inc(x_ready, 1)
                    elif s[0] == "yp":
                        wait(dve, m_read, n, NM, MU["yT"])
                        link(v.tensor_copy(yh[:], xT[:]), n, per)
                        v.tensor_tensor(yl[:], xT[:], yh[:], ALU.subtract).then_inc(yp_ready, 1)
                    elif s[0] == "logits":
                        wait(dve, m_ready, n, NM, MU["logits"])
                        v.tensor_tensor(rt[:, 0, :, :], M[:, 0:LT * EX].rearrange("p (t e) -> p t e", e=EX),
                                        brb[:].unsqueeze(1).to_broadcast([P, LT, EX]), ALU.add).then_inc(m_read, 1)
                        wait(dve, m_read, n, NM, MU["logits"])
                        less_maximum(P, LT, n, per, logits_ready)
                    elif s[0] == "top2":
                        wait(dve, ex_ready, n, 1, 1)
                        top2(P, LT, n, per).then_inc(cw_ready, 1)
                if any(s[0] == "norm" for s in r.plain):
                    assert links[0] - setup_links[0] == CHAIN, links[0] - setup_links[0]
                if r is r0:
                    setup_links[0] = links[0]

            rounds(dve, body)

        @block.tensor
        def _(pe):
            mm, tr = nc.tensor.matmul, nc.tensor.transpose
            pe.sem_inc(fin_ready, 1)

            def setup(k):
                if k == 0:
                    pe.wait_ge(consts_in, 16 * len(SMALL))
                    for h in range(H):
                        ins = mm(AC[:, h // 4, (h % 4) * P:(h % 4 + 1) * P], wqT[:, h, :], wkT[:, h, :],
                                 start=True, stop=True)
                    ins.then_inc(setup_pe, 1)
                    for h in range(H):
                        ins = mm(Y[:, h:h + 1], wkT[:, h, :], biasT[:, h:h + 1], start=True, stop=True)
                    ins.then_inc(setup_pe, 1)
                elif k == 1:
                    pe.wait_ge(setup_dve, 1)
                    mm(M[:, 0:1], clsx[0:1, :], ident[0:1, 0:1], start=True, stop=True).then_inc(setup_pe, 1)
                elif k == 2:
                    pe.wait_ge(setup_dve, 3)
                    for h in range(H):
                        ins = mm(M[0:DK, h:h + 1], xT[:, h * DK:(h + 1) * DK], cc[:, XC:XC + 1], start=True, stop=True)
                    ins.then_inc(setup_pe, 1)
                elif k == 3:
                    pe.wait_ge(setup_dve, 4)
                    for h in range(H):
                        mm(M[:, h:h + 1], wqT[:, h, :], kc[:, h:h + 1], start=True, stop=True)
                    for h in range(H):
                        ins = mm(M[:, H + h:H + h + 1], (h1, h2)[h // 4][:, h % 4, :], cc[:, XC:XC + 1],
                                 start=True, stop=True)
                    ins.then_inc(setup_pe, 1)
                elif k == 4:
                    pe.wait_ge(setup_dve, 5)
                    mm(M[:, 0:1], urep, cc[:, XC:XC + 1], start=True, stop=True)
                    mm(M[:, 1:2], grep, cc[:, XC:XC + 1], start=True, stop=True).then_inc(setup_pe, 1)
                else:
                    pe.wait_ge(setup_dve, 6)

            def class_tokens(k):
                if k == 0:
                    pe.wait_ge(cls_dve, 1)
                    pe.wait_ge(m_read, B * NM)
                    tr(M[0:B, 0:P], colc[:], ident).then_inc(cls_pe, 1)
                elif k == 2:
                    pe.wait_ge(cls_dve, 2)
                    tr(M[:, 0:B], clsx[:], ident[0:B, 0:B]).then_inc(cls_pe, 1)
                elif k == 3:
                    pe.wait_ge(cls_dve, 3)
                    mm(M[0:B, 0:EX], xcT, wr[:], start=True, stop=True).then_inc(cls_pe, 1)
                    for ex in range(EX):
                        own = padded[:, ex * P:(ex + 1) * P]
                        mm(AC[:, 0, :], own, w1h[:, ex, :], start=ex == 0, stop=False)
                        ins = mm(AC[:, 0, :], own, w1l[:, ex, :], start=False, stop=ex == EX - 1)
                    ins.then_inc(cls_pe, 1)
                elif k == 4:
                    pe.wait_ge(cls_dve, 5)
                    for f in range(FB):
                        ins = mm(M[:, f * EX * B:(f + 1) * EX * B], gf[:, tile(f)], con[:, C_PAIR:C_PAIR + EX * B],
                                 start=True, stop=True)
                    ins.then_inc(cls_pe, 1)
                elif k == 5:
                    pe.wait_ge(cls_dve, 6)
                    mm(AC[:, 0, 0:EX * B], con[0:B, C_ONES:C_ONES + P], diag, start=True, stop=True)
                    tr(AC[0:EX, 0, EX * B:EX * B + B], rt[0:B, 0, 0, :], ident[0:B, 0:B]).then_inc(cls_pe, 1)
                elif k == 6:
                    pe.wait_ge(cls_dve, 7)
                    mm(M[0:B, 0:D], cwT[:, 0:B], b2e[:], start=True, stop=False)
                    for c in range(EX * FB):
                        f, ex = divmod(c, EX)
                        hid = slice(c * B, (c + 1) * B)
                        ins = three(M[0:B, 0:D], (hidh[:, hid], hidl[:, hid]),
                                    (w2h[:, ex, tile(f)], w2l[:, ex, tile(f)]), False, c == EX * FB - 1)
                    ins.then_inc(cls_pe, 1)

            def three(out, a, b, start, stop):
                mm(out, a[0], b[0], start=start, stop=False)
                mm(out, a[0], b[1], start=False, stop=False)
                return mm(out, a[1], b[0], start=False, stop=stop)

            def tile(t):
                return slice(t * P, (t + 1) * P)

            def use(r, s):
                r, s = r.used(s)
                kind, i = s
                es = r.eslot(s)
                r.wait_e(pe, parts_ready, s)
                h, l_ = eh[:, es, :], el[:, es, :]
                if kind == "exp":
                    at, t = divmod(i, LT)
                    if t == 0:
                        wait(pe, ac_read[at % 2], r.n1, 3, at // 2)
                    g = t * ATT + at
                    ins = three(AC[0:C + 1, at % 2, :], (v1h[:, g, 0:C + 1], v1l[:, g, 0:C + 1]), (h, l_),
                                t == 0, t == LT - 1)
                elif kind == "tanh":
                    head, t = divmod(i, LT)
                    if head % 4 == 0 and t == 0:
                        wait(pe, ac_read[head // 4], r.n, 3, 2)
                        wait(pe, vz_ready, r.n, 1, 1)
                    mm(AC[:, head // 4, :], vz[:, t, head, :], h, start=head % 4 == 0 and t == 0, stop=False)
                    ins = mm(AC[:, head // 4, :], vz[:, t, head, :], l_, start=False,
                             stop=head % 4 == 3 and t == LT - 1)
                else:
                    ex, f = divmod(i, FB)
                    if f == 0:
                        wait(pe, prod_ready, r.batch(i), EX, ex - (r.batch(i) == B - 1 and ex > 0))
                        wait(pe, out_ready, r.batch(i), 1, 0)
                    ins = three(output_of(r.batch(i), ex), (w2h[:, ex, tile(f)], w2l[:, ex, tile(f)]), (h, l_),
                                f == 0, f == FB - 1)
                ins.then_inc(parts_used, 1)

            def body(r):
                n, n1, m = r.n, r.n1, r.m
                for s in r.steps:
                    kind, i = s[0], s[1]
                    if kind == "use":
                        use(r, s)
                        continue
                    if kind == "setup":
                        setup(i)
                    if kind == "clp":
                        class_tokens(i)
                    if kind in W_KINDS:
                        r.wait_read(pe, s, before=1)
                        slot = r.slot(s)
                    if kind == "k":
                        if r is r0:
                            pe.wait_ge(first_in, 16 * len(FIRST))
                        wait(pe, xin_ready, n1, 16, 16)
                        mm(W[:, slot, :], wqk[:, P:2 * P], xin[:], start=True, stop=True).then_inc(w_ready, 1)
                    elif kind == "q":
                        mm(W[:, slot, :], wqk[:, 0:P], xin[:], start=True, stop=True).then_inc(w_ready, 1)
                    elif kind == "v":
                        for k in range(2):
                            ins = mm(W[:, slot, k * ATT * C:(k + 1) * ATT * C], xin[:, tile(2 * i + k)], wv[:],
                                     start=True, stop=True)
                        ins.then_inc(w_ready, 1)
                    elif kind == "max":
                        t, at = divmod(i, ATT)
                        if i == 0:
                            wait(pe, kz_ready, n1, 1, 1)
                            r.wait_read(pe, ("q", 0))
                        mm(W[:, slot, :], qs[:, tile(t)], kz[:, at, :], start=True, stop=True).then_inc(w_ready, 1)
                    elif kind == "shift":
                        wait(pe, shift_ready, n1, 1, 1)
                        for t in range(LT):
                            ins = mm(W[:, slot, tile(t)], nm[:, t, :], ident, start=True, stop=True)
                        ins.then_inc(w_ready, 1)
                    elif kind == "exp":
                        at, t = divmod(i, LT)
                        if i == 0:
                            r.wait_read(pe, ("shift", 0))
                            r.wait_read(pe, ("v", 1))
                        mm(W[:, slot, :], kz[:, at, tile(t)], qs[:], start=True, stop=True).then_inc(w_ready, 1)
                    elif kind == "norm":
                        for k in range(2):
                            wait(pe, ac_read[k], n, 3, 2)
                        for at in range(ATT):
                            ins = tr(W[:, slot, at * (C + 1):(at + 1) * (C + 1)], ot[0:C + 1, at, tile(i)],
                                     ident[0:C + 1, 0:C + 1])
                        ins.then_inc(w_ready, 1)
                    elif kind == "xT":
                        wait(pe, m_read, n, NM, 0)
                        wait(pe, x_ready, n, 2, 1)
                        for t in range(LT):
                            ins = tr(M[:, tile(t)], x[:, t, :], ident)
                        ins.then_inc(m_ready, 1)
                    elif kind == "tk":
                        wait(pe, m_read, n, NM, MU["xT"])
                        wait(pe, xp_ready, n, 1, 1)
                        three(M[:], (rreph[:], rrepl[:]), (xh[:], xl[:]), True, True).then_inc(m_ready, 1)
                    elif kind == "tq":
                        wait(pe, m_read, n, NM, MU["tk"])
                        three(M[:], (greph[:], grepl[:]), (xh[:], xl[:]), True, True).then_inc(m_ready, 1)
                    elif kind == "g":
                        wait(pe, m_read, n, NM, MU["g"] + i - 1)
                        three(M[:], (mh[:, i, :], ml[:, i, :]), (xh[:], xl[:]), True, True).then_inc(m_ready, 1)
                    elif kind == "tanh":
                        h, t = divmod(i, LT)
                        wait(pe, g_ready, n, H, h + 1)
                        three(W[:, slot, :], (xh[:, tile(t)], xl[:, tile(t)]), (gh[:, h % 2, :], gl[:, h % 2, :]),
                              True, True).then_inc(w_ready, 1)
                    elif kind == "mix":
                        for k in range(2):
                            wait(pe, ac_read[k], n, 3, 3)
                        wait(pe, ck_ready, n, 1, 1)
                        wait(pe, m_read, n, NM, MU["mix"] - 1)
                        for t in range(LT):
                            mm(M[:, tile(t)], AT[:, 0, tile(t)], con[:, C_SEL:C_SEL + P], start=True, stop=False)
                            mm(M[:, tile(t)], AT[:, 1, tile(t)], con[:, C_SEL + P:C_SEL + 2 * P], start=False, stop=False)
                            ins = mm(M[:, tile(t)], tk[:, tile(t)], con[:, C_HALF:C_HALF + P], start=False, stop=True)
                        ins.then_inc(m_ready, 1)
                    elif kind == "yT":
                        wait(pe, x_ready, n, 2, 2)
                        for t in range(LT):
                            ins = tr(M[:, tile(t)], x[:, t, :], ident)
                        ins.then_inc(m_ready, 1)
                    elif kind == "logits":
                        wait(pe, m_read, n, NM, MU["yT"])
                        for t in range(LT):
                            ins = mm(M[:, t * EX:(t + 1) * EX], xT[:, tile(t)], wr[:], start=True, stop=True)
                        ins.then_inc(m_ready, 1)
                    elif kind == "cwT":
                        wait(pe, cw_ready, n, 1, 1)
                        for t in range(LT):
                            ins = tr(M[0:EX, tile(t)], rt[:, 0, t, :], ident)
                        ins.then_inc(m_ready, 1)
                    elif kind == "relu":
                        ex, f = divmod(i, FB)
                        if i == 0:
                            wait(pe, yp_ready, n, 1, 1)
                            pe.wait_ge(wts_lo, 2 * EX)
                        three(W[:, slot, :], (w1h[:, ex, tile(f)], w1l[:, ex, tile(f)]), (yh[:], yl[:]), True, True
                              ).then_inc(w_ready, 1)
                    elif kind == "fin":
                        wait(pe, acc_added, m, EX, EX)
                        for t in range(LT):
                            ins = tr(Y[:, tile(t)], acc[:, tile(t)], ident)
                        ins.then_inc(fin_ready, 1)

            rounds(pe, body)


def kernel(**inputs):
    import concourse.bacc as _bacc
    from concourse.bass_utils import run_bass_kernel_spmd as _run

    i = {k: np.asarray(v) for k, v in inputs.items()}
    f4 = np.float32

    def tok(k):
        return i[f"L0_tok_w{k}"]

    wqk, wv = np.zeros((D, 2 * P), f4), np.zeros((D, ATT * C), f4)
    for a, (q, k, v, sq, sk) in enumerate(((1, 2, 3, 0, 0), (4, 5, 6, 0, 1), (7, 8, 9, 1, 1), (10, 11, 12, 1, 0))):
        for rep in range(3):
            c0 = a * ROWS + rep * DQ
            wqk[sq * C:(sq + 1) * C, c0:c0 + DQ] = tok(q)
            wqk[sk * C:(sk + 1) * C, P + c0:P + c0 + DQ] = tok(k)
        wv[sk * C:(sk + 1) * C, a * C:(a + 1) * C] = tok(v)
    xT = i["x"].transpose(0, 3, 2, 1).reshape(B, D, L)
    Wq, Wk = i["L0_attn_Wq"], i["L0_attn_Wk"]
    W1, W2, b1, b2 = i["L0_ffn_W1"], i["L0_ffn_W2"], i["L0_ffn_b1"], i["L0_ffn_b2"]
    arrays = {
        "consts": constants(),
        "wqk": wqk,
        "wv": wv,
        "wqT": Wq.T.reshape(H, DK, D).transpose(1, 0, 2),
        "wkT": Wk.T.reshape(H, DK, D).transpose(1, 0, 2),
        "wk": Wk,
        "wr": i["L0_ffn_Wr"],
        "brb": np.broadcast_to(i["L0_ffn_br"], (P, EX)),
        "ag": np.broadcast_to(np.concatenate([i["L0_tok_alpha"], i["L0_tok_gamma"]]), (P, 2)),
        "b1T": b1.reshape(EX, FB, P).transpose(2, 0, 1).reshape(P, EX * FB),
        "b2T": b2.T,
        "b2": b2,
        "biasT": i["L0_attn_rel_content_bias"].reshape(H, DK).T,
        "cls": np.broadcast_to(i["cls_tok"].reshape(1, D), (B, D)),
        "xT": np.concatenate([xT, xT[-1:]]),
        "w1": W1.transpose(1, 0, 2),
        "w2": W2.reshape(EX, FB, P, D).transpose(2, 0, 1, 3).reshape(P, EX, F),
    }
    arrays = {k: np.ascontiguousarray(a) for k, a in arrays.items()}
    nc = _bacc.Bacc("TRN2", target_bir_lowering=False, num_devices=1)
    A = {k: nc.dram_tensor(f"in_{k}", a.shape, F32, kind="ExternalInput").ap() for k, a in arrays.items()}
    A["out"] = nc.dram_tensor("out_0", (B, L + 1, D), F32, kind="ExternalOutput").ap()
    build(nc, A)
    r = _run(nc, [{f"in_{k}": a for k, a in arrays.items()}], core_ids=[0])
    return r.results[0]["out_0"]
```
